# Optimizing a Trainium2 kernel written in Bass

```python
import numpy as np
import jax
import jax.numpy as jnp

def _softmax(x, axis=-1):
    return jax.nn.softmax(x, axis=axis)

def _gelu(x):
    return jax.nn.gelu(x, approximate=True)

def _silu(x):
    return jax.nn.silu(x)

def _sigmoid(x):
    return jax.nn.sigmoid(x)

def _layernorm(x, axis=-1, eps=1e-05):
    m = jnp.mean(x, axis=axis, keepdims=True)
    v = jnp.var(x, axis=axis, keepdims=True)
    return (x - m) / jnp.sqrt(v + eps)

def _scatter_add(tgt, idx, src, axis=0):
    return tgt.at[idx].add(src)

def _segment_sum(src, seg, n):
    return jax.ops.segment_sum(src, seg, n)
kernel_name = 'mk_vit_tower_cls_d1_tok_img1024_r4_4debcc'

def setup_inputs(seed: int=0):
    np.random.seed(seed)
    _w = jnp.asarray

    def _rec_inputs():
        import jax
        import jax.numpy as jnp
        _rk = jax.random.key(seed)
        x = 7.22013e-05 + 1.00017 * jax.random.normal(jax.random.fold_in(_rk, 1), (4, 1, 512, 256), jnp.float32)
        cls_tok = 0.02 * jax.random.normal(jax.random.fold_in(_rk, 5), (1, 1, 256), jnp.float32)
        return (x, cls_tok)
    x, cls_tok = _rec_inputs()

    def _L0_tok_setup():
        import jax, jax.numpy as jnp
        import numpy as np
        import math
        EMBED_DIM = 256
        NUM_HEADS = 16
        HEAD_DIM = EMBED_DIM // NUM_HEADS
        INPUT_DIM = 256
        key = jax.random.key(seed)
        k_x, k_wqkv, k_wout = jax.random.split(key, 3)
        x = jax.random.normal(k_x, (4, 1, 512, INPUT_DIM), dtype=jnp.float32)

        def xavier(k, shape):
            fan_out, fan_in = shape
            bound = math.sqrt(6.0 / (fan_in + fan_out))
            return jax.random.uniform(k, shape, jnp.float32, -bound, bound)
        w_qkv = xavier(k_wqkv, (3 * EMBED_DIM, INPUT_DIM))
        b_qkv = jnp.zeros((3 * EMBED_DIM,), jnp.float32)
        w_out = xavier(k_wout, (EMBED_DIM, EMBED_DIM))
        b_out = jnp.zeros((EMBED_DIM,), jnp.float32)
        return {'x': x, 'w_qkv': w_qkv, 'b_qkv': b_qkv, 'w_out': w_out, 'b_out': b_out}
    _L0_tok_all = _L0_tok_setup()
    _L0_tok_in = {k: v for k, v in _L0_tok_all.items() if k in ('w_qkv', 'b_qkv', 'w_out', 'b_out')}
    del _L0_tok_all

    def _L0_attn_setup():
        import math
        import jax, jax.numpy as jnp
        import numpy as np
        N_HEADS = 8
        EPS = 1e-05
        key = jax.random.key(seed)
        ks = jax.random.split(key, 5)
        B, L, D = (4, 512, 256)
        w_scale = 0.02
        return {'x': jax.random.normal(ks[0], (B, L, D), dtype=jnp.float32), 'Wq': jax.random.normal(ks[1], (D, D), dtype=jnp.float32) * w_scale, 'Wk': jax.random.normal(ks[2], (D, D), dtype=jnp.float32) * w_scale, 'Wv': jax.random.normal(ks[3], (D, D), dtype=jnp.float32) * w_scale, 'Wo': jax.random.normal(ks[4], (D, D), dtype=jnp.float32) * w_scale, 'gn_weight': jnp.ones((D,), dtype=jnp.float32), 'gn_bias': jnp.zeros((D,), dtype=jnp.float32)}
    _L0_attn_all = _L0_attn_setup()
    _L0_attn_in = {k: v for k, v in _L0_attn_all.items() if k in ('Wq', 'Wk', 'Wv', 'Wo', 'gn_weight', 'gn_bias')}
    del _L0_attn_all

    def _L0_ffn_setup():
        import jax, jax.numpy as jnp
        import numpy as np
        D_MODEL, D_FF, RANK = (256, 1024, 64)
        B, S = (4, 1024)
        key = jax.random.key(seed)
        ks = jax.random.split(key, 7)
        return {'x': jax.random.normal(ks[0], (B, S, D_MODEL), dtype=jnp.float32), 'U1': jax.random.normal(ks[1], (D_MODEL, RANK), dtype=jnp.float32) * 0.02, 'V1': jax.random.normal(ks[2], (RANK, D_FF), dtype=jnp.float32) * 0.02, 'b1': jnp.zeros((D_FF,), dtype=jnp.float32), 'U2': jax.random.normal(ks[3], (D_FF, RANK), dtype=jnp.float32) * 0.02, 'V2': jax.random.normal(ks[4], (RANK, D_MODEL), dtype=jnp.float32) * 0.02, 'b2': jnp.zeros((D_MODEL,), dtype=jnp.float32)}
    _L0_ffn_all = _L0_ffn_setup()
    _L0_ffn_in = {k: v for k, v in _L0_ffn_all.items() if k in ('U1', 'V1', 'b1', 'U2', 'V2', 'b2')}
    del _L0_ffn_all
    return {'x': x, 'cls_tok': cls_tok, 'L0_tok_w_qkv': _L0_tok_in['w_qkv'], 'L0_tok_b_qkv': _L0_tok_in['b_qkv'], 'L0_tok_w_out': _L0_tok_in['w_out'], 'L0_tok_b_out': _L0_tok_in['b_out'], 'L0_attn_Wq': _L0_attn_in['Wq'], 'L0_attn_Wk': _L0_attn_in['Wk'], 'L0_attn_Wv': _L0_attn_in['Wv'], 'L0_attn_Wo': _L0_attn_in['Wo'], 'L0_attn_gn_weight': _L0_attn_in['gn_weight'], 'L0_attn_gn_bias': _L0_attn_in['gn_bias'], 'L0_ffn_U1': _L0_ffn_in['U1'], 'L0_ffn_V1': _L0_ffn_in['V1'], 'L0_ffn_b1': _L0_ffn_in['b1'], 'L0_ffn_U2': _L0_ffn_in['U2'], 'L0_ffn_V2': _L0_ffn_in['V2'], 'L0_ffn_b2': _L0_ffn_in['b2']}

def reference(x, cls_tok, L0_tok_w_qkv, L0_tok_b_qkv, L0_tok_w_out, L0_tok_b_out, L0_attn_Wq, L0_attn_Wk, L0_attn_Wv, L0_attn_Wo, L0_attn_gn_weight, L0_attn_gn_bias, L0_ffn_U1, L0_ffn_V1, L0_ffn_b1, L0_ffn_U2, L0_ffn_V2, L0_ffn_b2):
    import jax
    import jax.numpy as jnp

    def _L0_tok_ref(x, w_qkv, b_qkv, w_out, b_out):
        import jax, jax.numpy as jnp
        import numpy as np
        import math
        EMBED_DIM = 256
        NUM_HEADS = 16
        HEAD_DIM = EMBED_DIM // NUM_HEADS
        INPUT_DIM = 256
        B, y, S, _ = x.shape
        qkv = jnp.einsum('bysd,ed->byse', x, w_qkv) + b_qkv
        qkv = qkv.reshape(B, S, NUM_HEADS, 3 * HEAD_DIM).transpose(0, 2, 1, 3)
        q, k, v = jnp.split(qkv, 3, axis=-1)
        logits = jnp.einsum('bhqd,bhkd->bhqk', q, k) / math.sqrt(HEAD_DIM)
        attn = jax.nn.softmax(logits, axis=-1)
        vals = jnp.einsum('bhqk,bhkd->bhqd', attn, v)
        vals = vals.transpose(0, 2, 1, 3).reshape(B, S, EMBED_DIM)
        return jnp.einsum('bse,oe->bso', vals, w_out) + b_out

    def _L0_attn_ref(x, Wq, Wk, Wv, Wo, gn_weight, gn_bias):
        import math
        import jax, jax.numpy as jnp
        import numpy as np
        N_HEADS = 8
        EPS = 1e-05
        B, L, D = x.shape
        H = N_HEADS
        dh = D // H
        gammas = 1.0 - jnp.exp(jnp.linspace(math.log(1.0 / 32.0), math.log(1.0 / 512.0), H)).astype(x.dtype)

        def proj(W):
            return (x @ W.T).reshape(B, L, H, dh).transpose(1, 0, 2, 3)
        qT, kT, vT = (proj(Wq), proj(Wk), proj(Wv))
        g = gammas[None, :, None, None]

        def step(S, qkv_t):
            q_t, k_t, v_t = qkv_t
            S = g * S + k_t[..., :, None] * v_t[..., None, :]
            y_t = jnp.einsum('bhde,bhd->bhe', S, q_t)
            return (S, y_t)
        S0 = jnp.zeros((B, H, dh, dh), dtype=x.dtype)
        _, ys = jax.lax.scan(step, S0, (qT, kT, vT))
        out = ys.transpose(1, 0, 2, 3)
        mean = out.mean(axis=(1, 3), keepdims=True)
        var = out.var(axis=(1, 3), keepdims=True)
        out = (out - mean) * jax.lax.rsqrt(var + EPS)
        out = out.reshape(B, L, D) * gn_weight + gn_bias
        return out @ Wo.T

    def _L0_ffn_ref(x, U1, V1, b1, U2, V2, b2):
        import jax, jax.numpy as jnp
        import numpy as np
        D_MODEL, D_FF, RANK = (256, 1024, 64)
        B, S = (4, 1024)
        P = jnp.einsum('bsd,dr->bsr', x, U1)
        H = jax.nn.gelu(jnp.einsum('bsr,rf->bsf', P, V1) + b1)
        Q = jnp.einsum('bsf,fr->bsr', H, U2)
        return jnp.einsum('bsr,rd->bsd', Q, V2) + b2
    h = _L0_tok_ref(x, L0_tok_w_qkv, L0_tok_b_qkv, L0_tok_w_out, L0_tok_b_out)
    h = jnp.concatenate([jnp.broadcast_to(cls_tok, (h.shape[0], 1, h.shape[2])), h], axis=1)
    h = h + _L0_attn_ref(_layernorm(h, axis=-1), L0_attn_Wq, L0_attn_Wk, L0_attn_Wv, L0_attn_Wo, L0_attn_gn_weight, L0_attn_gn_bias)
    h = h + _L0_ffn_ref(_layernorm(h, axis=-1), L0_ffn_U1, L0_ffn_V1, L0_ffn_b1, L0_ffn_U2, L0_ffn_V2, L0_ffn_b2)
    return h

_drawn_inputs = setup_inputs


def setup_inputs(seed=0):
    import zlib

    import numpy as np

    out = dict(_drawn_inputs(seed))
    spreads = {'L0_tok_b_qkv': (0.0, 0.1),
     'L0_tok_b_out': (0.0, 0.1),
     'L0_attn_gn_weight': (1.0, 0.2),
     'L0_attn_gn_bias': (0.0, 0.1),
     'L0_ffn_b1': (0.0, 0.568),
     'L0_ffn_b2': (0.0, 0.1)}
    factors = {'cls_tok': 5.879,
     'L0_ffn_U1': 7.173,
     'L0_ffn_V1': 7.835,
     'L0_ffn_U2': 3.486,
     'L0_ffn_V2': 3.808}
    for name, (base, spread) in spreads.items():
        noise = np.random.default_rng([zlib.crc32(name.encode()), seed]).standard_normal(out[name].shape)
        drawn = base * np.exp(spread * noise) if base else spread * noise
        out[name] = jnp.asarray(drawn.astype(out[name].dtype))
    for name, factor in factors.items():
        out[name] = (out[name] * factor).astype(out[name].dtype)
    return out
```

```python
from contextlib import ExitStack

import concourse.bass as bass
from concourse import mybir

ALU = mybir.AluOpType
ACT = mybir.ActivationFunctionType
F32 = mybir.dt.float32
BF16 = mybir.dt.bfloat16
AX = mybir.AxisListType.X

B, S, D = 4, 512, 256
P = 128
QT = S // P
KC = D // P
NH, HD = 16, 16
HG = 4
NG = NH // HG
STEPS = NH * QT
GS = HG * QT
HH = NH // 2
PARTS = 6
KR = PARTS * HD
KM = KR + 2
Q_PART = [0, 0, 1, 1, 0, 2]
K_PART = [0, 1, 0, 1, 2, 0]
RH, RD = 8, 32
RQ = 4
RANK, FF = 64, 1024
FT = FF // P
EPS = 1e-5
AHEAD = 20
PV_LAG = 3

FRONT = [("wq", KC * D), ("wk", KC * D), ("wv", KC * D), ("qbias", KC), ("kbias", KC), ("vbias", D), ("ident", P)]
REST = [("wout", KC * D), ("bout", D), ("rwq", KC * D), ("rwk", KC * D), ("rwv", KC * D), ("rwo", KC * D),
        ("gq", KC * S), ("gk", KC * S), ("causal", P), ("blocks", P), ("headmean", P), ("gnw", KC), ("gnb", KC),
        ("u1", KC * P), ("b1", FT), ("u2", FT * RANK), ("v2", D), ("b2", D)]

AT = {
    "FQ0": 9, "FQ1": 10, "FK0": 24, "FK1": 25, "FV0": 26, "FV1": 27,
    "VT0": 5, "VT1": 6, "OP0": 7, "OP1": 8, "HT0": 11, "HT1": 13, "RQ0": 14, "RQ1": 15, "RK0": 16, "RK1": 17,
    "RV0": 18, "RV1": 19, "KT0": 21, "KT1": 22, "KV0": 23, "KV1": 29,
    "RA0": 30, "RA1": 37, "GM": 43, "GV": 45, "WO0": 47, "WO1": 48, "HU0": 51, "HU1": 53, "U1": 54,
    "H0": 56, "H1": 56, "H2": 57, "H3": 57, "H4": 58, "H5": 58, "H6": 59, "H7": 59, "U2": 62, "V0": 63, "V1": 63,
}
FRONT_STAGES = ("FQ0", "FQ1", "FK0", "FK1", "FV0", "FV1")
CLS_START = ("C0", "C1", "C2", "C3", "C4")
CLS_END = {"CW": 49, "CT": 52, "CU": 55, "CH": 60, "CQ": 62, "CV": 63}


def stages(it):
    out = []
    for t in range(STEPS):
        step = STEPS * it + t
        if t == 0 and it == 0:
            out += [(t, name, 0) for name in CLS_START]
        if step >= GS + 4 and (step - GS - 4) % GS == 0 and (step - GS - 4) // GS < B * NG:
            out.append((t, "NR", (step - GS - 4) // GS))
        for name, at in AT.items():
            if at != t:
                continue
            if name in FRONT_STAGES:
                if 0 <= it + 1 < B:
                    out.append((t, name, it + 1))
            elif 0 <= it - 1 < B:
                if name in ("RA0", "RA1"):
                    out += [(t, "A" + name[2] + "0", it - 1)]
                else:
                    out.append((t, name, it - 1))
            if name in ("RA0", "RA1"):
                pass
        for ft in range(2):
            if 0 <= it - 1 < B and 0 < t - AT[f"RA{ft}"] <= 4:
                c = t - AT[f"RA{ft}"]
                if c < 4:
                    out.append((t, f"A{ft}{c}", it - 1))
                out.append((t, f"Y{ft}{c - 1}", it - 1))
        if it == B:
            out += [(t, name, 0) for name, at in CLS_END.items() if at == t]
        if (step + 4) % GS == 0 and 0 <= (step + 4) // GS < B * NG:
            out.append((t, "MT", (step + 4) // GS))
    return out


def repeat(ap, axis, n):
    shape = list(ap.shape)
    shape[axis] = n
    return ap.broadcast_to(shape)


def offsets(pack):
    at, out = 0, {}
    for name, n in pack:
        out[name] = slice(at, at + n)
        at += n
    return out, at


def vit_tower(nc, xt, front, rest, v1, cls, out):
    foff, fcols = offsets(FRONT)
    roff, rcols = offsets(REST)

    use = {}
    for it in range(-1, B + 1):
        for _, name, b in stages(it):
            key = (name[:2], b) if name[0] == "Y" else (name, b)
            if key not in use:
                use[key] = (len(use) % 3, len(use) // 3)

    with ExitStack() as ctx:
        def sb(name, shape, dt=F32):
            return ctx.enter_context(nc.sbuf_tensor(name, shape, dt))

        def sem(name):
            return ctx.enter_context(nc.semaphore(name))

        fpack = sb("fpack", [P, fcols])
        rpack = sb("rpack", [P, rcols])

        def w(name, split=None):
            ap = fpack[:, foff[name]] if name in foff else rpack[:, roff[name]]
            return ap.rearrange("p (a b) -> p a b", a=split) if split else ap

        wq, wk, wv = w("wq", KC), w("wk", KC), w("wv", KC)
        wout, rwq, rwk, rwv, rwo = w("wout", KC), w("rwq", KC), w("rwk", KC), w("rwv", KC), w("rwo", KC)
        gq, gk = w("gq", KC), w("gk", KC)
        u1, u2 = w("u1", KC), w("u2", FT)
        ident = w("ident")
        identb = sb("identb", [P, P], BF16)
        v1p = sb("v1p", [P, 3, FF], BF16)
        xT = sb("xT", [P, KC, S])
        qkf = sb("qkf", [P, KC, S])
        split = sb("split", [P, 2, 3, KC, S], BF16)
        qr = sb("qr", [KM, NH, S], BF16)
        kr = sb("kr", [KM, NH, S], BF16)
        vstage = sb("vstage", [P, QT, D])
        vaug = sb("vaug", [P, QT, NH, 32])
        probs = sb("probs", [P, QT, HG, S])
        negmax = sb("negmax", [P, 2, GS])
        mparts = sb("mparts", [P, 2, GS], BF16)
        mrows = sb("mrows", [2 * GS, P], BF16)
        oT = sb("oT", [P, S])
        rsum = sb("rsum", [P, QT, HG])
        vals = sb("vals", [P, QT, D])
        h = sb("h", [P, QT, D])
        hn = sb("hn", [P, QT, D])
        hT = sb("hT", [P, KC, S])
        bst = sb("bst", [P, QT, 6])
        mv = sb("mv", [P, QT, 2])
        rstd = sb("rstd", [P, QT])
        mhalf = sb("mhalf", [P, QT])
        hbias = sb("hbias", [P, 2, KC])
        qblk = sb("qblk", [P, KC, RQ, S])
        state = sb("state", [P, KC, 4, P])
        zc = sb("zc", [P, KC, B])
        gst = sb("gst", [P, KC, 2, 6])
        gmv = sb("gmv", [P, KC, 2])
        gmu = sb("gmu", [P, KC])
        gd = sb("gd", [P, KC])
        gvar = sb("gvar", [P, KC])
        grs = sb("grs", [P, KC])
        gscale = sb("gscale", [P, KC])
        gshift = sb("gshift", [P, KC])
        pA = sb("pA", [P, S], BF16)
        pB = sb("pB", [P, S], BF16)
        pr = sb("pr", [P, S])
        qT = pr
        hid = sb("hid", [P, FT, S])
        v1f = hid[:, 2:4, :].rearrange("p a b -> p (a b)")
        rqT, rkT = hid[:, 0:2, :], hid[:, 2:4, :]
        rv = hid[:, 4:6, :].rearrange("p a (c n) -> p (a c) n", n=D)
        ktok = hid[:, 6:8, :].rearrange("p a (c n) -> p (a c) n", n=D)
        amask = qkf[:, :, :].rearrange("p a (j n) -> p a j n", j=RQ)
        y = sb("y", [P, KC, S + 1])
        kvm = y[:, :, 0:3 * P].rearrange("p f (c n) -> p f c n", c=3)
        z = sb("z", [P, KC, S + 1])
        vT = z[:, :, 0:S]
        clsrow = sb("clsrow", [B, D])
        crow = sb("crow", [B, 4, D])
        cst = sb("cst", [B, 6])
        cmv = sb("cmv", [B, 4])
        cT = sb("cT", [P, 2, KC, B])
        one = sb("one", [P, 1])
        cP = sb("cP", [P, B])
        cA = sb("cA", [P, 2, B], BF16)
        chid = sb("chid", [P, FT, B])
        cQ = sb("cQ", [P, B])

        st_ps = ctx.enter_context(nc.psum_tensor("st_ps", [P, 2, S], F32))
        mx_ps = ctx.enter_context(nc.psum_tensor("mx_ps", [P, 2, S], F32))
        pv_ps = ctx.enter_context(nc.psum_tensor("pv_ps", [P, S], F32))
        ps = [ctx.enter_context(nc.psum_tensor(f"ps{i}", [P, S], F32)) for i in range(3)]

        front_in, rest_in, cls_in = sem("front_in"), sem("rest_in"), sem("cls_in")
        x_in = sem("x_in")
        full = [sem(f"full{i}") for i in range(3)]
        drained = [sem(f"drained{i}") for i in range(3)]
        max_full, max_done = sem("max_full"), sem("max_done")
        st_full, exp_done = sem("st_full"), sem("exp_done")
        pv_done, o_ready = sem("pv_done"), sem("o_ready")
        m_split, m_rows = sem("m_split"), sem("m_rows")
        qk_parts = sem("qk_parts")
        rep = [sem("rep0"), sem("rep1")]
        v_half = sem("v_half")
        ln_stats, ln_done = sem("ln_stats"), sem("ln_done")
        hb_done = sem("hb_done")
        qblk_in = sem("qblk_in")
        states = sem("states")
        y_chunk = sem("y_chunk")
        g_mean, g_dev, g_scale, z_done, zc_done = sem("g_mean"), sem("g_dev"), sem("g_scale"), sem("z_done"), sem("zc_done")
        p_rest, p_parts = sem("p_rest"), sem("p_parts")
        gelu_done = sem("gelu_done")
        out_done = sem("out_done")
        consts, vconst = sem("consts"), sem("vconst")
        ones_done, zeros_done = sem("ones_done"), sem("zeros_done")
        c_hn, c_rstd, c_row, c_gelu, c_out, c_var = (sem("c_hn"), sem("c_rstd"), sem("c_row"), sem("c_gelu"),
                                                       sem("c_out"), sem("c_var"))
        c_cp = sem("c_cp")
        v_chain, p_chain = sem("v_chain"), sem("p_chain")

        def bank(key):
            return ps[use[key][0]]

        def wait_full(eng, key):
            i, n = use[key]
            eng.wait_ge(full[i], n + 1)

        def wait_drained(eng, key):
            i, n = use[key]
            eng.wait_ge(drained[i], n + 1)

        def wait_free(pe, key):
            i, n = use[key]
            if n:
                pe.wait_ge(drained[i], n)

        def inc_full(ins, key):
            ins.then_inc(full[use[key][0]], 1)

        def inc_drained(ins, key):
            ins.then_inc(drained[use[key][0]], 1)

        vcount, pcount = [0], [0]

        def vlink(ins):
            vcount[0] += 1
            ins.then_inc(v_chain, 1)
            nc.vector.wait_ge(v_chain, vcount[0])

        def plink(ins):
            pcount[0] += 1
            ins.then_inc(p_chain, 1)
            nc.gpsimd.wait_ge(p_chain, pcount[0])

        walk = [(it, t, STEPS * it + t, [(n, b) for u, n, b in stages(it) if u == t])
                for it in range(-1, B + 1) for t in range(STEPS)]
        block = ctx.enter_context(nc.Block())

        @block.sync
        def _(sp):
            sp.dma_start(fpack[:, :], front).then_inc(front_in, 16)
            sp.dma_start(xT[:, :, :], xt[0]).then_inc(x_in, 16)
            sp.dma_start(clsrow[:, :], cls).then_inc(cls_in, 16)
            sp.dma_start(rpack[:, :], rest).then_inc(rest_in, 16)
            sp.dma_start(v1f, v1).then_inc(rest_in, 16)
            for it, t, step, todo in walk:
                for half in range(2):
                    b = it + 1 - half
                    if not (t == (32 if half == 0 else 0) and 0 <= b < B):
                        continue
                    sp.wait_ge(qk_parts, 2 * (b + 1))
                    if b:
                        sp.wait_ge(st_full, STEPS * b - (STEPS // 2 if half == 0 else 0))
                    for g in range(PARTS):
                        for i, (dst, part) in enumerate(((qr, Q_PART), (kr, K_PART))):
                            sp.dma_start(dst[HD * g:HD * (g + 1), HH * half:HH * (half + 1), :],
                                         split[:, i, part[g], half, :]).then_inc(rep[half], 16)
                for name, b in todo:
                    if name == "MT":
                        wait_drained(sp, (name, b))
                        if b >= NG:
                            sp.wait_ge(st_full, GS * (b - NG + 1))
                        g = b % NG
                        for i in range(2):
                            sp.dma_start(qr[KR + i:KR + i + 1, HG * g:HG * (g + 1), :],
                                         mrows[GS * i:GS * (i + 1), :]).then_inc(m_rows, 16)
                    if name == "FV1" and b + 1 < B:
                        wait_full(sp, (name, b))
                        sp.dma_start(xT[:, :, :], xt[b + 1]).then_inc(x_in, 16)
                    if name == "RQ1":
                        wait_drained(sp, ("RQ0", b))
                        wait_drained(sp, ("RQ1", b))
                        sp.wait_ge(zeros_done, 1)
                        if b:
                            wait_full(sp, ("A13", b - 1))
                        for j in range(RQ):
                            sp.dma_start(qblk[RD * j:RD * (j + 1), :, j, :],
                                         rqT[RD * j:RD * (j + 1), :, :]).then_inc(qblk_in, 16)
                    if name in ("V0", "V1"):
                        i = int(name[1])
                        wait_drained(sp, (name, b))
                        sp.dma_start(out[b, 1 + i * 2 * P:1 + (i + 1) * 2 * P, :].rearrange("(a p) n -> p a n", p=P),
                                     hn[:, 2 * i:2 * i + 2, :]).then_inc(out_done, 16)
                    if name == "CV":
                        sp.wait_ge(c_out, 1)
                        sp.dma_start(out[:, 0, :], crow[:, 2, :]).then_inc(out_done, 16)
            sp.wait_ge(out_done, 16 * (2 * B + 1))

        @block.tensor
        def _(pe):
            def mm(o, a, b, start, stop, check=False):
                return nc.tensor.matmul(o, a, b, start=start, stop=stop, skip_group_check=check)

            def tokens_out(key, lhs, weights, i):
                o = bank(key)
                for a in range(2):
                    for k in range(KC):
                        last = mm(o[:, a * D:(a + 1) * D], lhs[:, k, (2 * i + a) * P:(2 * i + a + 1) * P],
                                  weights[:, k, :], k == 0, k == KC - 1)
                inc_full(last, key)

            def features_out(key, weights, rhs, ft):
                o = bank(key)
                for k in range(KC):
                    last = mm(o[:, :], weights[:, k, ft * P:(ft + 1) * P], rhs[:, k, :], k == 0, k == KC - 1)
                inc_full(last, key)

            def transposes(key, src, ft):
                o = bank(key)
                for q in range(QT):
                    last = nc.tensor.transpose(o[:, q * P:(q + 1) * P], src[:, q, ft * P:(ft + 1) * P], ident)
                inc_full(last, key)

            def stage(name, b):
                key = (name[:2], b) if name[0] == "Y" else (name, b)
                if name[0] != "Y" or name[2] == "0":
                    wait_free(pe, key)
                o = bank(key)
                if name == "MT":
                    pe.wait_ge(m_split, b + 1)
                    pe.wait_ge(consts, 3)
                    inc_full(nc.tensor.transpose(o[:, 0:P // 2].bitcast(BF16)[0:2 * GS, :],
                                                 mparts[:, :, :].rearrange("p a b -> p (a b)"), identb[:, :]), key)
                elif name == "NR":
                    pe.wait_ge(o_ready, b + 1)
                    for q in range(QT):
                        last = nc.tensor.transpose(o[:, q * P:(q + 1) * P], oT[:, q * P:(q + 1) * P], ident)
                    inc_full(last, key)
                elif name in ("FQ0", "FQ1", "FK0", "FK1"):
                    if name == "FQ0":
                        pe.wait_ge(front_in, 16)
                        pe.wait_ge(x_in, 16 * (b + 1))
                    features_out(key, wq if name[1] == "Q" else wk, xT, int(name[2]))
                elif name in ("FV0", "FV1"):
                    tokens_out(key, xT, wv, int(name[2]))
                elif name in ("VT0", "VT1"):
                    if name == "VT0":
                        wait_drained(pe, ("NR", NG * b + NG - 1))
                    transposes(key, vals, int(name[2]))
                elif name in ("OP0", "OP1"):
                    if name == "OP0":
                        pe.wait_ge(rest_in, 32)
                        wait_drained(pe, ("VT0", b))
                        wait_drained(pe, ("VT1", b))
                    tokens_out(key, vT, wout, int(name[2]))
                elif name in ("HT0", "HT1", "HU0", "HU1"):
                    if name[2] == "0":
                        pe.wait_ge(ln_done, 2 * b + (1 if name[1] == "T" else 2))
                    transposes(key, hn, int(name[2]))
                elif name in ("RQ0", "RQ1", "RK0", "RK1"):
                    if name == "RQ0":
                        wait_drained(pe, ("HT0", b))
                        wait_drained(pe, ("HT1", b))
                    features_out(key, rwq if name[1] == "Q" else rwk, hT, int(name[2]))
                elif name in ("RV0", "RV1"):
                    tokens_out(key, hT, rwv, int(name[2]))
                elif name in ("KT0", "KT1"):
                    if name == "KT0":
                        wait_drained(pe, ("RK0", b))
                        wait_drained(pe, ("RK1", b))
                    for a, c in enumerate(range(2) if name == "KT0" else range(2, 3)):
                        for ft in range(KC):
                            last = nc.tensor.transpose(o[:, a * D + ft * P:a * D + (ft + 1) * P],
                                                       rkT[:, ft, c * P:(c + 1) * P], ident)
                    inc_full(last, key)
                elif name in ("KV0", "KV1"):
                    ft = int(name[2])
                    if ft == 0:
                        for n in ("RV0", "RV1", "KT0", "KT1"):
                            wait_drained(pe, (n, b))
                    for c in range(3):
                        last = mm(o[:, c * P:(c + 1) * P], ktok[:, c, ft * P:(ft + 1) * P],
                                  rv[:, c, ft * P:(ft + 1) * P], True, True)
                    inc_full(last, key)
                elif name[0] == "A":
                    ft, c = int(name[1]), int(name[2])
                    if name == "A00":
                        pe.wait_ge(qblk_in, 64 * (b + 1))
                    inc_full(mm(o[:, :], rkT[:, ft, c * P:(c + 1) * P], qblk[:, ft, :, c * P:(c + 1) * P], True, True), key)
                elif name[0] == "Y":
                    ft, c = int(name[1]), int(name[2])
                    if name == "Y00":
                        pe.wait_ge(states, b + 1)
                    at = slice(c * P, (c + 1) * P)
                    mm(o[:, at], state[:, ft, c, :], rqT[:, ft, at], True, False, True)
                    wait_drained(pe, (f"A{ft}{c}", b))
                    for j in range(RQ):
                        last = mm(o[RD * j:RD * (j + 1), at], rv[:, c, ft * P + RD * j:ft * P + RD * (j + 1)],
                                  amask[:, c % 2, j, :], False, True, True)
                    if c == 3:
                        inc_full(last, key)
                    else:
                        last.then_inc(y_chunk, 1)
                elif name == "GM":
                    pe.wait_ge(g_mean, b + 1)
                    inc_full(mm(o[:, 0:KC], w("headmean"), gmv[:, :, 0], True, True), key)
                elif name == "GV":
                    pe.wait_ge(g_dev, b + 1)
                    inc_full(mm(o[:, 0:KC], w("headmean"), gd[:, :], True, True), key)
                elif name in ("WO0", "WO1"):
                    if name == "WO0":
                        pe.wait_ge(z_done, KC * (b + 1))
                    tokens_out(key, z, rwo, int(name[2]))
                elif name == "U1":
                    wait_drained(pe, ("HU0", b))
                    wait_drained(pe, ("HU1", b))
                    features_out(key, u1, hT, 0)
                elif name[0] == "H":
                    f = int(name[1])
                    if f == 0:
                        pe.wait_ge(p_parts, b + 1)
                        wait_drained(pe, ("U1", b))
                    at = slice(f * P, (f + 1) * P)
                    mm(o[:, :], v1p[:, 0, at], pA[:, :], True, False)
                    mm(o[:, :], v1p[:, 1, at], pA[:, :], False, False)
                    inc_full(mm(o[:, :], v1p[:, 2, at], pB[:, :], False, True), key)
                elif name == "U2":
                    for f in range(FT):
                        if f % (FT // 2) == 0:
                            pe.wait_ge(gelu_done, 2 * b + 1 + f // (FT // 2))
                        i = f % 2
                        last = mm(o[RANK * i:RANK * (i + 1), :], u2[:, f, :], hid[:, f, :], f < 2, f >= FT - 2, True)
                    inc_full(last, key)
                elif name in ("V0", "V1"):
                    i = int(name[1])
                    if i == 0:
                        wait_drained(pe, ("U2", b))
                    for a in range(2):
                        last = mm(o[:, a * D:(a + 1) * D], qT[:, (2 * i + a) * P:(2 * i + a + 1) * P], w("v2"), True, True)
                    inc_full(last, key)
                elif name == "C0":
                    pe.wait_ge(c_hn, 1)
                    for k in range(KC):
                        last = mm(o[:, k:k + 1], crow[0:1, 0, k * P:(k + 1) * P], one[0:1, :], True, True)
                    inc_full(last, key)
                elif name == "C1":
                    wait_drained(pe, ("C0", 0))
                    pe.wait_ge(rest_in, 32)
                    for ft in range(KC):
                        for k in range(KC):
                            last = mm(o[:, ft:ft + 1], rwq[:, k, ft * P:(ft + 1) * P], cT[:, 0, k, 0:1], k == 0, k == KC - 1)
                    inc_full(last, key)
                elif name == "C2":
                    for i, weights in enumerate((rwk, rwv)):
                        for k in range(KC):
                            last = mm(o[0:1, i * D:(i + 1) * D], cT[:, 0, k, 0:1], weights[:, k, :], k == 0, k == KC - 1)
                    inc_full(last, key)
                elif name == "C3":
                    wait_drained(pe, ("C2", 0))
                    for ft in range(KC):
                        at = slice(ft * P, (ft + 1) * P)
                        last = mm(o[:, at], crow[0:1, 1, at], crow[0:1, 2, at], True, True)
                    inc_full(last, key)
                elif name == "C4":
                    wait_drained(pe, ("C1", 0))
                    wait_drained(pe, ("C3", 0))
                    for ft in range(KC):
                        last = mm(o[:, ft:ft + 1], state[:, ft, 0, :], cT[:, 1, ft, 0:1], True, True)
                    inc_full(last, key)
                elif name == "CW":
                    pe.wait_ge(zc_done, B)
                    for k in range(KC):
                        last = mm(o[0:B, 0:D], zc[:, k, :], rwo[:, k, :], k == 0, k == KC - 1)
                    inc_full(last, key)
                elif name == "CT":
                    pe.wait_ge(c_hn, 2)
                    for k in range(KC):
                        last = mm(o[:, k * B:(k + 1) * B], crow[0:B, 0, k * P:(k + 1) * P], w("ident")[0:B, 0:B], True, True)
                    inc_full(last, key)
                elif name == "CU":
                    wait_drained(pe, ("CT", 0))
                    for k in range(KC):
                        last = mm(o[:, 0:B], u1[:, k, :], cT[:, 0, k, :], k == 0, k == KC - 1)
                    inc_full(last, key)
                elif name == "CH":
                    wait_drained(pe, ("CU", 0))
                    pe.wait_ge(c_cp, 1)
                    for f in range(FT):
                        at = slice(f * P, (f + 1) * P)
                        mm(o[:, f * B:(f + 1) * B], v1p[:, 0, at], cA[:, 0, :], True, False)
                        mm(o[:, f * B:(f + 1) * B], v1p[:, 1, at], cA[:, 0, :], False, False)
                        last = mm(o[:, f * B:(f + 1) * B], v1p[:, 2, at], cA[:, 1, :], False, True)
                    inc_full(last, key)
                elif name == "CQ":
                    pe.wait_ge(c_gelu, 1)
                    for f in range(FT):
                        i = f % 2
                        last = mm(o[RANK * i:RANK * (i + 1), 0:B], u2[:, f, :], chid[:, f, :], f < 2, f >= FT - 2, True)
                    inc_full(last, key)
                elif name == "CV":
                    wait_drained(pe, ("CQ", 0))
                    inc_full(mm(o[0:B, 0:D], cQ[:, :], w("v2"), True, True), key)
                else:
                    raise ValueError(name)

            for it, t, step, todo in walk:
                m = step + AHEAD
                if 0 <= m < B * STEPS:
                    head, q = m % STEPS // QT, m % QT
                    if m % STEPS in (0, STEPS // 2):
                        pe.wait_ge(rep[m % STEPS // (STEPS // 2)], 16 * 2 * PARTS * (m // STEPS + 1))
                    if m >= 2:
                        pe.wait_ge(max_done, m - 1)
                    mm(mx_ps[:, m % 2, :], qr[0:KR, head, q * P:(q + 1) * P], kr[0:KR, head, :], True, True)\
                        .then_inc(max_full, 1)
                if 0 <= step < B * STEPS:
                    n, kt, j = step // GS, step % GS // HG, step % HG
                    head = HG * (n % NG) + j
                    if step % GS == 0:
                        pe.wait_ge(m_rows, 32 * (n + 1))
                        pe.wait_ge(ones_done, 1)
                    if step >= 2:
                        pe.wait_ge(exp_done, step - 1)
                    mm(st_ps[:, step % 2, :], kr[:, head, kt * P:(kt + 1) * P], qr[:, head, :], True, True)\
                        .then_inc(st_full, 1)
                last_exp = step - PV_LAG
                if 0 <= last_exp < B * STEPS and last_exp % HG == HG - 1:
                    n, kt = last_exp // GS, last_exp % GS // HG
                    pe.wait_ge(exp_done, last_exp + 1)
                    if kt == 0 and n % (NG // 2) == 0:
                        pe.wait_ge(v_half, n // (NG // 2) + 1)
                    if kt == 0 and n:
                        pe.wait_ge(o_ready, n)
                    for j in range(HG):
                        last = mm(pv_ps[32 * j:32 * (j + 1), :], vaug[:, kt, HG * (n % NG) + j, :], probs[:, kt, j, :],
                                  kt == 0, kt == QT - 1)
                    last.then_inc(pv_done, 1)
                for name, b in todo:
                    stage(name, b)

        @block.scalar
        def _(act):
            def stage(name, b):
                key = (name, b)
                if name in ("FQ0", "FQ1", "FK0", "FK1"):
                    wait_full(act, key)
                    if name[2] == "0" and (b or name[1] == "K"):
                        act.wait_ge(qk_parts, 2 * b + (name[1] == "K"))
                    if name == "FQ0" and b == 0:
                        act.wait_ge(consts, 3)
                    bias = hbias[:, int(name[1] == "K"), :]
                    inc_drained(nc.scalar.activation(qkf[:, int(name[2]), :], bank(key)[:, :], ACT.Identity,
                                                     bias=bias[:, int(name[2]):int(name[2]) + 1], scale=0.5), key)
                elif name in ("VT0", "VT1"):
                    wait_full(act, key)
                    if b:
                        wait_full(act, ("OP1", b - 1))
                    inc_drained(nc.scalar.copy(vT[:, int(name[2]), :], bank(key)[:, :]), key)
                elif name in ("HT0", "HT1", "HU0", "HU1"):
                    wait_full(act, key)
                    if name[1] == "U":
                        wait_full(act, ("RV1", b))
                    elif b:
                        wait_full(act, ("U1", b - 1))
                    inc_drained(nc.scalar.copy(hT[:, int(name[2]), :], bank(key)[:, :]), key)
                elif name in ("RV0", "RV1"):
                    wait_full(act, key)
                    if b:
                        wait_full(act, ("Y1", b - 1))
                    i = int(name[2])
                    inc_drained(nc.scalar.copy(rv[:, 2 * i:2 * i + 2, :].rearrange("p a b -> p (a b)"), bank(key)[:, :]), key)
                elif name in ("KT0", "KT1"):
                    wait_full(act, key)
                    if b:
                        wait_full(act, ("KV1", b - 1))
                    c, n = (0, 2) if name == "KT0" else (2, 1)
                    inc_drained(nc.scalar.copy(ktok[:, c:c + n, :].rearrange("p a b -> p (a b)"), bank(key)[:, 0:n * D]), key)
                elif name in ("Y03", "Y13"):
                    ft = int(name[1])
                    wait_full(act, (name[:2], b))
                    if b:
                        act.wait_ge(z_done, KC * b)
                        act.wait_ge(g_mean, b)
                    inc_drained(nc.scalar.copy(y[:, ft, 0:S], bank((name[:2], b))[:, :]), (name[:2], b))
                elif name == "GV":
                    act.wait_ge(g_scale, b + 1)
                    if b:
                        wait_full(act, ("WO1", b - 1))
                        act.wait_ge(zc_done, b)
                    for ft in range(KC):
                        nc.scalar.activation(z[:, ft, :], y[:, ft, :], ACT.Identity, bias=gshift[:, ft:ft + 1],
                                             scale=gscale[:, ft:ft + 1]).then_inc(z_done, 1)
                elif name == "H7":
                    for i in range(2):
                        wait_drained(act, (f"H{4 * i + 3}", b))
                        wait_drained(act, (f"H{4 * i + 2}", b))
                        wait_drained(act, (f"H{4 * i + 1}", b))
                        nc.scalar.activation(hid[:, 4 * i:4 * i + 4, :], hid[:, 4 * i:4 * i + 4, :],
                                             ACT.Gelu_apprx_tanh).then_inc(gelu_done, 1)
                elif name == "U2":
                    wait_full(act, key)
                    if b:
                        wait_full(act, ("V1", b - 1))
                    inc_drained(nc.scalar.copy(qT[:, :], bank(key)[:, :]), key)
                elif name == "CH":
                    wait_drained(act, key)
                    nc.scalar.activation(chid[:, :, :], chid[:, :, :], ACT.Gelu_apprx_tanh).then_inc(c_gelu, 1)

            for it, t, step, todo in walk:
                if 0 <= step < B * STEPS:
                    n, kt, j = step // GS, step % GS // HG, step % HG
                    act.wait_ge(st_full, step + 1)
                    if n and j == 0:
                        act.wait_ge(pv_done, QT * (n - 1) + kt + 1)
                    nc.scalar.activation(probs[:, kt, j, :], st_ps[:, step % 2, :], ACT.Exp).then_inc(exp_done, 1)
                n = (step - PV_LAG) // GS
                if 0 <= n < B * NG and (step - PV_LAG) % GS == GS - 1:
                    act.wait_ge(pv_done, QT * (n + 1))
                    if n:
                        wait_full(act, ("NR", n - 1))
                    nc.scalar.copy(oT[:, :], pv_ps[:, :]).then_inc(o_ready, 1)
                for name, b in todo:
                    stage(name, b)

        @block.vector
        def _(dve):
            dve.wait_ge(front_in, 16)
            nc.vector.tensor_copy(identb[:, :], ident).then_inc(consts, 1)
            for i, name in enumerate(("qbias", "kbias")):
                nc.vector.tensor_scalar(hbias[:, i, :], w(name), 0.5, None, ALU.mult).then_inc(consts, 1)
            dve.wait_ge(cls_in, 16)

            def row_stats(src, n):
                vlink(nc.vector.bn_stats(cst[0:n, :], src))
                vlink(nc.vector.bn_aggr(cmv[0:n, 0:2], cst[0:n, :]))
                nc.vector.tensor_scalar(cmv[0:n, 2:3], cmv[0:n, 1:2], EPS, None, ALU.add).then_inc(c_var, 1)

            def row_norm(src, n, count):
                dve.wait_ge(c_rstd, count)
                nc.vector.tensor_scalar(crow[0:n, 0, :], src, cmv[0:n, 0:1], cmv[0:n, 3:4],
                                        ALU.subtract, ALU.mult).then_inc(c_hn, 1)

            row_stats(clsrow[0:1, :], 1)
            row_norm(clsrow[0:1, :], 1, 1)
            dve.wait_ge(rest_in, 32)
            vlink(nc.vector.tensor_copy(v1p[:, 0, :], v1f))
            vlink(nc.vector.tensor_tensor(hid[:, 0:2, :].rearrange("p a b -> p (a b)"), v1f, v1p[:, 0, :], ALU.subtract))
            vlink(nc.vector.tensor_copy(v1p[:, 1, :], hid[:, 0:2, :].rearrange("p a b -> p (a b)")))
            vlink(nc.vector.tensor_tensor(v1p[0:64, 2, :], hid[0:64, 0:2, :].rearrange("p a b -> p (a b)"),
                                          v1p[0:64, 1, :], ALU.subtract))
            vlink(nc.vector.tensor_copy(v1p[64:128, 2, :], v1p[64:128, 0, :]))

            def layer_norm_stats(b, count):
                for q in range(QT):
                    nc.vector.bn_stats(bst[:, q, :], h[:, q, :]).then_inc(v_chain, 1)
                vcount[0] += QT
                dve.wait_ge(v_chain, vcount[0])
                for q in range(QT):
                    nc.vector.bn_aggr(mv[:, q, :], bst[:, q, :]).then_inc(v_chain, 1)
                vcount[0] += QT
                dve.wait_ge(v_chain, vcount[0])
                nc.vector.tensor_scalar(rstd[:, :], mv[:, :, 1], EPS, None, ALU.add).then_inc(ln_stats, 1)

            def stage(name, b):
                key = (name, b)
                if name == "FQ1" or name == "FK1":
                    i = int(name[1] == "K")
                    wait_drained(dve, (name[:2] + "0", b))
                    wait_drained(dve, (name[:2] + "1", b))
                    if b:
                        for half in range(2):
                            dve.wait_ge(rep[half], 16 * 2 * PARTS * b)
                    vlink(nc.vector.tensor_copy(split[:, i, 0, :, :], qkf[:, :, :]))
                    vlink(nc.vector.tensor_tensor(qkf[:, :, :], qkf[:, :, :], split[:, i, 0, :, :], ALU.subtract))
                    vlink(nc.vector.tensor_copy(split[:, i, 1, :, :], qkf[:, :, :]))
                    nc.vector.tensor_tensor(split[:, i, 2, :, :], qkf[:, :, :], split[:, i, 1, :, :],
                                            ALU.subtract).then_inc(qk_parts, 1)
                elif name in ("FV0", "FV1"):
                    wait_full(dve, key)
                    if b:
                        dve.wait_ge(v_half, 2 * b)
                    i = int(name[2])
                    vb = repeat(w("vbias").rearrange("p (a n) -> p a n", a=1), 1, 2)
                    inc_drained(nc.vector.tensor_tensor(vstage[:, 2 * i:2 * i + 2, :],
                                                        bank(key)[:, :].rearrange("p (a n) -> p a n", a=2), vb, ALU.add), key)
                elif name == "MT":
                    wait_full(dve, key)
                    if b:
                        dve.wait_ge(m_rows, 32 * b)
                    inc_drained(nc.vector.tensor_copy(mrows[:, :], bank(key)[:, 0:P // 2].bitcast(BF16)[0:2 * GS, :]), key)
                elif name == "NR":
                    wait_full(dve, key)
                    g = b % NG
                    if b:
                        wait_drained(dve, ("NR", b - 1))
                    if g == 0 and b:
                        wait_full(dve, ("VT1", b // NG - 1))
                    o = bank(key)[:, :].rearrange("p (q j c) -> p q j c", q=QT, j=HG)
                    vlink(nc.vector.reciprocal(rsum[:, :, :], o[:, :, :, HD]))
                    r = repeat(rsum[:, :, :].rearrange("p q (j a) -> p q j a", a=1), 3, HD)
                    dst = vals[:, :, HG * HD * g:HG * HD * (g + 1)].rearrange("p q (j c) -> p q j c", j=HG)
                    inc_drained(nc.vector.tensor_tensor(dst, o[:, :, :, 0:HD], r, ALU.mult), key)
                elif name in ("OP0", "OP1"):
                    wait_full(dve, key)
                    i = int(name[2])
                    if b:
                        wait_drained(dve, ("V1", b - 1))
                        wait_drained(dve, ("V0", b - 1))
                    bb = repeat(w("bout").rearrange("p (a n) -> p a n", a=1), 1, 2)
                    inc_drained(nc.vector.tensor_tensor(h[:, 2 * i:2 * i + 2, :],
                                                        bank(key)[:, :].rearrange("p (a n) -> p a n", a=2), bb, ALU.add), key)
                    if i:
                        wait_drained(dve, ("OP0", b))
                        wait_drained(dve, ("OP1", b))
                        if b:
                            dve.wait_ge(ln_done, 2 * b)
                        layer_norm_stats(b, 2 * b + 1)
                elif name in ("RQ0", "RQ1", "RK0", "RK1"):
                    wait_full(dve, key)
                    ft = int(name[2])
                    if b:
                        wait_full(dve, ("Y1", b - 1))
                        dve.wait_ge(qblk_in, 64 * b)
                        if name[1] == "K":
                            wait_full(dve, ("A13", b - 1))
                    table, dst = (gq, rqT) if name[1] == "Q" else (gk, rkT)
                    inc_drained(nc.vector.tensor_tensor(dst[:, ft, :], bank(key)[:, :], table[:, ft, :], ALU.mult), key)
                elif name in ("KV0", "KV1"):
                    wait_full(dve, key)
                    if b:
                        dve.wait_ge(states, b)
                    ft = int(name[2])
                    mask = repeat(w("blocks").rearrange("p (a n) -> p a n", a=1), 1, 3)
                    inc_drained(nc.vector.tensor_tensor(kvm[:, ft, :, :],
                                                        bank(key)[:, 0:3 * P].rearrange("p (a n) -> p a n", a=3),
                                                        mask, ALU.mult), key)
                elif name[0] == "A":
                    ft, c = int(name[1]), int(name[2])
                    wait_full(dve, key)
                    if c >= 2:
                        dve.wait_ge(y_chunk, 3 * (2 * b + ft) + c - 1)
                    elif ft:
                        wait_full(dve, ("Y0", b))
                    else:
                        dve.wait_ge(qk_parts, 2 * min(b + 3, B))
                        if b:
                            wait_full(dve, ("Y1", b - 1))
                    mask = repeat(w("causal").rearrange("p (a n) -> p a n", a=1), 1, RQ)
                    inc_drained(nc.vector.tensor_tensor(amask[:, c % 2, :, :],
                                                        bank(key)[:, :].rearrange("p (a n) -> p a n", a=RQ),
                                                        mask, ALU.mult), key)
                elif name in ("Y03", "Y13"):
                    ft = int(name[1])
                    wait_drained(dve, (name[:2], b))
                    if b == 0 and ft == 0:
                        wait_drained(dve, ("C4", 0))
                    if b:
                        dve.wait_ge(g_dev, b)
                    half = (S + 2) // 2
                    nc.vector.bn_stats(gst[:, ft, 0, :], y[:, ft, 0:half]).then_inc(v_chain, 1)
                    nc.vector.bn_stats(gst[:, ft, 1, :], y[:, ft, half:S + 1]).then_inc(v_chain, 1)
                    vcount[0] += 2
                    dve.wait_ge(v_chain, vcount[0])
                    last = nc.vector.bn_aggr(gmv[:, ft, :], gst[:, ft, :, :].rearrange("p a b -> p (a b)"))
                    if ft:
                        last.then_inc(g_mean, 1)
                    else:
                        vlink(last)
                elif name == "GM":
                    wait_full(dve, key)
                    dve.wait_ge(g_mean, b + 1)
                    if b:
                        dve.wait_ge(g_scale, b)
                        wait_full(dve, ("GV", b - 1))
                    inc_drained(nc.vector.tensor_copy(gmu[:, :], bank(key)[:, 0:KC]), key)
                    wait_drained(dve, key)
                    vlink(nc.vector.tensor_tensor(gvar[:, :], gmv[:, :, 0], gmu[:, :], ALU.subtract))
                    vlink(nc.vector.tensor_tensor(gvar[:, :], gvar[:, :], gvar[:, :], ALU.mult))
                    nc.vector.tensor_tensor(gd[:, :], gvar[:, :], gmv[:, :, 1], ALU.add).then_inc(g_dev, 1)
                elif name == "GV":
                    wait_full(dve, key)
                    dve.wait_ge(g_dev, b + 1)
                    inc_drained(nc.vector.tensor_scalar(gvar[:, :], bank(key)[:, 0:KC], EPS, None, ALU.add), key)
                elif name in ("WO0", "WO1"):
                    wait_full(dve, key)
                    dve.wait_ge(ln_done, 2 * b + 1)
                    i = int(name[2])
                    hv = h[:, 2 * i:2 * i + 2, :].rearrange("p a b -> p (a b)")
                    inc_drained(nc.vector.tensor_tensor(hv, bank(key)[:, :], hv, ALU.add), key)
                    if i:
                        wait_drained(dve, ("WO0", b))
                        wait_drained(dve, ("WO1", b))
                        layer_norm_stats(b, 2 * b + 2)
                elif name == "U1":
                    wait_full(dve, key)
                    if b:
                        wait_full(dve, ("H7", b - 1))
                        dve.wait_ge(p_parts, b)
                    vlink(nc.vector.tensor_copy(pA[:, :], bank(key)[:, :]))
                    nc.vector.tensor_copy(pB[0:64, :], pA[0:64, :])
                    nc.vector.tensor_tensor(pr[:, :], bank(key)[:, :], pA[:, :], ALU.subtract)\
                        .then_inc(drained[use[key][0]], 1)
                elif name[0] == "H" and name[1].isdigit():
                    f = int(name[1])
                    wait_full(dve, key)
                    if b:
                        wait_full(dve, ("U2", b - 1))
                    inc_drained(nc.vector.tensor_scalar(hid[:, f, :], bank(key)[:, :], w("b1")[:, f:f + 1], None, ALU.add), key)
                elif name in ("V0", "V1"):
                    wait_full(dve, key)
                    dve.wait_ge(hb_done, b + 1)
                    wait_full(dve, ("HU1", b))
                    i = int(name[1])
                    inc_drained(nc.vector.tensor_tensor(hn[:, 2 * i:2 * i + 2, :].rearrange("p a b -> p (a b)"),
                                                        bank(key)[:, :], h[:, 2 * i:2 * i + 2, :].rearrange("p a b -> p (a b)"),
                                                        ALU.add), key)
                elif name == "C0":
                    wait_full(dve, key)
                    inc_drained(nc.vector.tensor_copy(cT[:, 0, :, 0], bank(key)[:, 0:KC]), key)
                elif name == "C1":
                    wait_full(dve, key)
                    inc_drained(nc.vector.tensor_copy(cT[:, 1, :, 0], bank(key)[:, 0:KC]), key)
                elif name == "C2":
                    wait_full(dve, key)
                    inc_drained(nc.vector.tensor_copy(crow[0:1, 1:3, :].rearrange("p a b -> p (a b)"), bank(key)[0:1, :]), key)
                elif name == "C3":
                    wait_full(dve, key)
                    mask = repeat(w("blocks").rearrange("p (a n) -> p a n", a=1), 1, KC)
                    inc_drained(nc.vector.tensor_tensor(state[:, :, 0, :],
                                                        bank(key)[:, 0:KC * P].rearrange("p (a n) -> p a n", a=KC),
                                                        mask, ALU.mult), key)
                elif name == "C4":
                    wait_full(dve, key)
                    inc_drained(nc.vector.tensor_copy(y[:, :, S], bank(key)[:, 0:KC]), key)
                elif name == "CW":
                    wait_full(dve, key)
                    wait_full(dve, ("C0", 0))
                    inc_drained(nc.vector.tensor_tensor(crow[:, 3, :], bank(key)[0:B, 0:D], clsrow[:, :], ALU.add), key)
                    wait_drained(dve, key)
                    dve.wait_ge(c_hn, 1)
                    row_stats(crow[:, 3, :], B)
                    row_norm(crow[:, 3, :], B, 2)
                elif name == "CT":
                    wait_full(dve, key)
                    wait_full(dve, ("C2", 0))
                    inc_drained(nc.vector.tensor_copy(cT[:, 0, :, :].rearrange("p a b -> p (a b)"), bank(key)[:, 0:KC * B]), key)
                elif name == "CU":
                    wait_full(dve, key)
                    vlink(nc.vector.tensor_copy(cA[:, 0, :], bank(key)[:, 0:B]))
                    vlink(nc.vector.tensor_copy(cA[0:64, 1, :], cA[0:64, 0, :]))
                    inc_drained(nc.vector.tensor_tensor(cP[:, :], bank(key)[:, 0:B], cA[:, 0, :], ALU.subtract), key)
                    wait_drained(dve, key)
                    vlink(nc.vector.tensor_copy(cA[64:128, 0, :], cP[64:128, :]))
                    nc.vector.tensor_tensor(cA[64:128, 1, :], cP[64:128, :], cA[64:128, 0, :], ALU.subtract).then_inc(c_cp, 1)
                elif name == "CH":
                    wait_full(dve, key)
                    bb = repeat(w("b1").rearrange("p (f a) -> p f a", a=1), 2, B)
                    inc_drained(nc.vector.tensor_tensor(chid[:, :, :], bank(key)[:, 0:FT * B].rearrange("p (f a) -> p f a", a=B),
                                                        bb, ALU.add), key)
                elif name == "CQ":
                    wait_full(dve, key)
                    inc_drained(nc.vector.tensor_copy(cQ[:, :], bank(key)[:, 0:B]), key)
                elif name == "CV":
                    wait_full(dve, key)
                    vlink(nc.vector.tensor_tensor(crow[:, 1, :], bank(key)[0:B, 0:D], crow[:, 3, :], ALU.add))
                    nc.vector.tensor_tensor(crow[:, 2, :], crow[:, 1, :], w("b2")[0:B, :], ALU.add).then_inc(c_out, 1)

            for it, t, step, todo in walk:
                m = step + AHEAD
                if 0 <= m < B * STEPS:
                    n = m // GS
                    dve.wait_ge(max_full, m + 1)
                    if n >= 2 and m % GS == 0:
                        dve.wait_ge(m_split, n - 1)
                    nc.vector.tensor_reduce(negmax[:, n % 2, m % GS:m % GS + 1], mx_ps[:, m % 2, :], AX, ALU.max,
                                            negate=True).then_inc(max_done, 1)
                    if m % GS == GS - 1:
                        dve.wait_ge(max_done, m + 1)
                        if n:
                            wait_full(dve, ("MT", n - 1))
                        vlink(nc.vector.tensor_copy(mparts[:, 0, :], negmax[:, n % 2, :]))
                        nc.vector.tensor_tensor(mparts[:, 1, :], negmax[:, n % 2, :], mparts[:, 0, :],
                                                ALU.subtract).then_inc(m_split, 1)
                for name, b in todo:
                    stage(name, b)

        @block.gpsimd
        def _(pool):
            nc.gpsimd.memset(kr[KR:KM, :, :], 1.0).then_inc(ones_done, 1)
            pool.wait_ge(ones_done, 1)
            nc.gpsimd.memset(mhalf[:, :], -0.5).then_inc(p_chain, 1)
            nc.gpsimd.memset(one[:, :], 1.0).then_inc(p_chain, 1)
            pcount[0] += 2
            nc.gpsimd.memset(vaug[:, :, :, HD:32], 0.0).then_inc(vconst, 1)
            pool.wait_ge(vconst, 1)
            nc.gpsimd.memset(vaug[:, :, :, HD:HD + 1], 1.0).then_inc(vconst, 1)
            nc.gpsimd.memset(qblk[:, :, :, :], 0.0).then_inc(zeros_done, 1)

            def class_rstd(n, count):
                pool.wait_ge(c_var, count)
                pool.wait_ge(p_chain, 2)
                nc.gpsimd.tensor_tensor(cmv[0:n, 3:4], cmv[0:n, 2:3], mhalf[0:n, 0:1], ALU.pow).then_inc(c_rstd, 1)

            def layer_norm(b, count):
                pool.wait_ge(ln_stats, count)
                plink(nc.gpsimd.tensor_tensor(rstd[:, :], rstd[:, :], mhalf[:, :], ALU.pow))
                for q in range(QT):
                    last = nc.gpsimd.tensor_scalar(hn[:, q, :], h[:, q, :], mv[:, q, 0:1], rstd[:, q:q + 1],
                                                   ALU.subtract, ALU.mult)
                    if q < QT - 1:
                        last.then_inc(p_chain, 1)
                        pcount[0] += 1
                last.then_inc(ln_done, 1)

            class_rstd(1, 1)
            for it, t, step, todo in walk:
                for half in range(2):
                    b = it + 1 - half
                    if t == (40 if half == 0 else 4) and 0 <= b < B:
                        wait_drained(pool, ("FV0", b))
                        wait_drained(pool, ("FV1", b))
                        pool.wait_ge(vconst, 2)
                        if b:
                            pool.wait_ge(pv_done, QT * (NG * b - (NG // 2 if half == 0 else 0)))
                        heads = slice(HH * half, HH * (half + 1))
                        nc.gpsimd.tensor_scalar(vaug[:, :, heads, 0:HD],
                                                vstage[:, :, HH * HD * half:HH * HD * (half + 1)]
                                                .rearrange("p q (h d) -> p q h d", d=HD), 1.0, None, ALU.mult)\
                            .then_inc(v_half, 1)
                for name, b in todo:
                    if name == "OP1":
                        if b:
                            pool.wait_ge(out_done, 32 * b)
                        layer_norm(b, 2 * b + 1)
                    elif name == "KV1":
                        wait_drained(pool, ("KV0", b))
                        wait_drained(pool, ("KV1", b))
                        wait_drained(pool, ("C3", 0))
                        if b:
                            wait_full(pool, ("Y1", b - 1))
                        for c in range(3):
                            ins = nc.gpsimd.tensor_tensor(state[:, :, c + 1, :], state[:, :, c, :], kvm[:, :, c, :], ALU.add)
                            if c < 2:
                                plink(ins)
                            else:
                                ins.then_inc(states, 1)
                    elif name == "GV":
                        wait_drained(pool, ("GV", b))
                        if b:
                            pool.wait_ge(z_done, KC * b)
                        plink(nc.gpsimd.tensor_tensor(grs[:, :], gvar[:, :], mhalf[:, 0:KC], ALU.pow))
                        plink(nc.gpsimd.tensor_tensor(gscale[:, :], grs[:, :], w("gnw"), ALU.mult))
                        plink(nc.gpsimd.tensor_tensor(grs[:, :], gmu[:, :], gscale[:, :], ALU.mult))
                        nc.gpsimd.tensor_tensor(gshift[:, :], w("gnb"), grs[:, :], ALU.subtract).then_inc(g_scale, 1)
                        pool.wait_ge(z_done, KC * (b + 1))
                        nc.gpsimd.tensor_scalar(zc[:, :, b], z[:, :, S], 1.0, None, ALU.mult).then_inc(zc_done, 1)
                    elif name == "WO1":
                        wait_full(pool, ("HT1", b))
                        layer_norm(b, 2 * b + 2)
                        pool.wait_ge(ln_done, 2 * b + 2)
                        bb = repeat(w("b2").rearrange("p (a n) -> p a n", a=1), 1, QT)
                        nc.gpsimd.tensor_tensor(h[:, :, :], h[:, :, :], bb, ALU.add).then_inc(hb_done, 1)
                    elif name == "U1":
                        wait_drained(pool, (name, b))
                        pool.wait_ge(hb_done, b + 1)
                        plink(nc.gpsimd.tensor_scalar(pA[64:128, :], pr[64:128, :], 1.0, None, ALU.mult))
                        if b:
                            wait_full(pool, ("H7", b - 1))
                        nc.gpsimd.tensor_tensor(pB[64:128, :], pr[64:128, :], pA[64:128, :], ALU.subtract).then_inc(p_parts, 1)
                        pool.wait_ge(p_parts, b + 1)
                    elif name == "CW":
                        class_rstd(B, 2)


def kernel(**inputs):
    import numpy as np
    import concourse.bacc as bacc
    from concourse.bass_utils import run_bass_kernel_spmd as run

    a = {k: np.asarray(v) for k, v in inputs.items()}
    f32 = np.float32

    def tiles(m):
        return np.ascontiguousarray(m.reshape(-1, P, m.shape[1]).transpose(1, 0, 2)).reshape(P, -1)

    def column(v):
        return np.ascontiguousarray(v.reshape(-1, P).T)

    def everywhere(v):
        return np.broadcast_to(v, (P, v.size))

    wqkv = a["L0_tok_w_qkv"].reshape(2, HH, 3, HD, D)
    bqkv = a["L0_tok_b_qkv"].reshape(2, HH, 3, HD)
    pick = lambda i: (wqkv[:, :, i].transpose(0, 2, 1, 3).reshape(D, D).T, bqkv[:, :, i].transpose(0, 2, 1).reshape(D))
    (wq, bq), (wk, bk) = pick(0), pick(1)
    wv, bv = wqkv[:, :, 2].reshape(D, D).T, bqkv[:, :, 2].reshape(D)
    v = {
        "wq": tiles(wq), "wk": tiles(wk), "wv": tiles(wv), "qbias": column(bq), "kbias": column(bk),
        "vbias": everywhere(bv), "ident": np.eye(P, dtype=f32),
        "wout": tiles(a["L0_tok_w_out"].T), "bout": everywhere(a["L0_tok_b_out"]),
        "rwq": tiles(a["L0_attn_Wq"].T), "rwk": tiles(a["L0_attn_Wk"].T), "rwv": tiles(a["L0_attn_Wv"].T),
        "rwo": tiles(a["L0_attn_Wo"].T), "gnw": column(a["L0_attn_gn_weight"]), "gnb": column(a["L0_attn_gn_bias"]),
        "u1": tiles(np.concatenate([a["L0_ffn_U1"]] * 2, axis=1)), "b1": column(a["L0_ffn_b1"]), "u2": tiles(a["L0_ffn_U2"]), "v2": np.concatenate([a["L0_ffn_V2"]] * 2),
        "b2": everywhere(a["L0_ffn_b2"]),
    }
    decay = (f32(1) - np.exp(np.linspace(np.log(1 / 32), np.log(1 / 512), RH).astype(f32))).astype(np.float64)
    pos = np.arange(1, S + 1)
    power = np.repeat(decay, RD)[:, None] ** pos[None]
    v["gq"], v["gk"] = tiles(power.astype(f32)), tiles((1 / power).astype(f32))
    i = np.arange(P)
    v["causal"] = (i[:, None] <= i[None]).astype(f32)
    v["blocks"] = (i[:, None] // RD == i[None] // RD).astype(f32)
    v["headmean"] = v["blocks"] * f32(1 / RD)
    arrays = {
        "xt": np.ascontiguousarray(a["x"].reshape(B, S, KC, P).transpose(0, 3, 2, 1)),
        "front": np.concatenate([v[n] for n, _ in FRONT], axis=1),
        "rest": np.concatenate([v[n] for n, _ in REST], axis=1),
        "v1": np.concatenate([a["L0_ffn_V1"]] * 2),
        "cls": np.ascontiguousarray(np.broadcast_to(a["cls_tok"].reshape(1, D), (B, D))),
    }
    nc = bacc.Bacc("TRN2", target_bir_lowering=False, num_devices=1)
    args = [nc.dram_tensor(n, m.shape, mybir.dt.from_np(m.dtype), kind="ExternalInput").ap() for n, m in arrays.items()]
    out = nc.dram_tensor("out_0_dram", (B, S + 1, D), F32, kind="ExternalOutput").ap()
    vit_tower(nc, *args, out)
    return run(nc, [arrays], core_ids=[0]).results[0]["out_0_dram"]
```

```python
from contextlib import ExitStack

import concourse.bass as bass
from concourse import mybir

ALU = mybir.AluOpType
ACT = mybir.ActivationFunctionType
F32 = mybir.dt.float32
BF16 = mybir.dt.bfloat16
AX = mybir.AxisListType.X

B, S, D = 4, 512, 256
P = 128
QT = S // P
KC = D // P
NH, HD = 16, 16
HG = 4
NG = NH // HG
STEPS = NH * QT
GS = HG * QT
HH = NH // 2
PARTS = 6
KR = PARTS * HD
KM = KR + 2
Q_PART = [0, 0, 1, 1, 0, 2]
K_PART = [0, 1, 0, 1, 2, 0]
RH, RD = 8, 32
RQ = 4
RANK, FF = 64, 1024
FT = FF // P
EPS = 1e-5
AHEAD = 20
PV_LAG = 3

FRONT = [("wq", KC * D), ("wk", KC * D), ("wv", KC * D), ("qbias", KC), ("kbias", KC), ("vbias", D), ("ident", P)]
REST = [("wout", KC * D), ("bout", D), ("rwq", KC * D), ("rwk", KC * D), ("rwv", KC * D), ("rwo", KC * D),
        ("gq", KC * S), ("gk", KC * S), ("causal", P), ("blocks", P), ("headmean", P), ("gnw", KC), ("gnb", KC),
        ("u1", KC * P), ("b1", FT), ("u2", FT * RANK), ("v2", D), ("b2", D)]

AT = {
    "FQ0": 10, "FK0": 10, "FQ1": 14, "FK1": 14, "FV0": 22, "FV1": 22,
    "VT0": 6, "VT1": 6, "OP0": 8, "OP1": 8, "HT0": 13, "HT1": 13, "RQ0": 16, "RQ1": 16, "RK0": 17, "RK1": 17,
    "RV0": 18, "RV1": 18, "KT0": 21, "KT1": 21, "KV0": 23, "KV1": 23,
    "RA0": 26, "RA1": 29, "GM": 33, "GV": 35, "WO0": 38, "WO1": 38, "HU0": 45, "HU1": 45, "U1": 48,
    "H0": 53, "H1": 53, "H2": 53, "H3": 53, "H4": 53, "H5": 53, "H6": 53, "H7": 53, "U2": 54, "V0": 57, "V1": 57,
}
FRONT_STAGES = ("FQ0", "FK0", "FQ1", "FK1", "FV0", "FV1", "SQ0", "SK0", "SQ1", "SK1")
BESIDE = {"SQ0": 11, "SK0": 12, "SQ1": 15, "SK1": 16, "LA": 9, "SS": 24, "GZ": 36, "LB": 39}
CHUNKS = [("A0", "A1"), ("Y0", "A2", "Y1", "A3"), ("Y2", "Y3")]
CLS_START = {30: "C0", 35: "C1", 36: "C2", 41: "C3", 46: "C4"}
CLS_END = {"CW": 39, "CT": 46, "CU": 47, "CH": 53, "CQ": 55, "CV": 58}


def stages(it):
    out = []
    for t in range(STEPS):
        step = STEPS * it + t
        if it == 0 and t in CLS_START:
            out.append((t, CLS_START[t], 0))
        if step >= GS + 4 and (step - GS - 4) % GS == 0 and (step - GS - 4) // GS < B * NG:
            out.append((t, "NR", (step - GS - 4) // GS))
        for name, at in (*AT.items(), *BESIDE.items()):
            if at != t:
                continue
            if name in FRONT_STAGES:
                if 0 <= it + 1 < B:
                    out.append((t, name, it + 1))
            elif 0 <= it - 1 < B and name not in ("RA0", "RA1"):
                out.append((t, name, it - 1))
        for ft in range(2):
            if 0 <= it - 1 < B and 0 <= t - AT[f"RA{ft}"] < len(CHUNKS):
                out += [(t, f"{n[0]}{ft}{n[1]}", it - 1) for n in CHUNKS[t - AT[f"RA{ft}"]]]
        if it == B:
            out += [(t, name, 0) for name, at in CLS_END.items() if at == t]
        if (step + 4) % GS == 0 and 0 <= (step + 4) // GS < B * NG:
            out.append((t, "MT", (step + 4) // GS))
    return out


def repeat(ap, axis, n):
    shape = list(ap.shape)
    shape[axis] = n
    return ap.broadcast_to(shape)


def offsets(pack):
    at, out = 0, {}
    for name, n in pack:
        out[name] = slice(at, at + n)
        at += n
    return out, at


def vit_tower(nc, xt, front, rest, v1, cls, out):
    foff, fcols = offsets(FRONT)
    roff, rcols = offsets(REST)

    use = {}
    for it in range(-1, B + 1):
        for _, name, b in stages(it):
            key = (name[:2], b) if name[0] == "Y" else (name, b)
            if key not in use and name not in BESIDE:
                use[key] = (len(use) % 3, len(use) // 3)

    with ExitStack() as ctx:
        def sb(name, shape, dt=F32):
            return ctx.enter_context(nc.sbuf_tensor(name, shape, dt))

        def sem(name):
            return ctx.enter_context(nc.semaphore(name))

        fpack = sb("fpack", [P, fcols])
        rpack = sb("rpack", [P, rcols])

        def w(name, split=None):
            ap = fpack[:, foff[name]] if name in foff else rpack[:, roff[name]]
            return ap.rearrange("p (a b) -> p a b", a=split) if split else ap

        wq, wk, wv = w("wq", KC), w("wk", KC), w("wv", KC)
        wout, rwq, rwk, rwv, rwo = w("wout", KC), w("rwq", KC), w("rwk", KC), w("rwv", KC), w("rwo", KC)
        gq, gk = w("gq", KC), w("gk", KC)
        u1, u2 = w("u1", KC), w("u2", FT)
        ident = w("ident")
        identb = sb("identb", [P, P], BF16)
        v1p = sb("v1p", [P, 3, FF], BF16)
        xT = sb("xT", [P, KC, S])
        qkf = sb("qkf", [P, KC, S])
        split = sb("split", [P, 2, 3, KC, S], BF16)
        qr = sb("qr", [KM, NH, S], BF16)
        kr = sb("kr", [KM, NH, S], BF16)
        vstage = sb("vstage", [P, QT, D])
        vaug = sb("vaug", [P, QT, NH, 32])
        probs = sb("probs", [P, QT, HG, S])
        negmax = sb("negmax", [P, 2, GS])
        mparts = sb("mparts", [P, 2, GS], BF16)
        mrows = sb("mrows", [2 * GS, P], BF16)
        oT = sb("oT", [P, S])
        rsum = sb("rsum", [P, QT, HG])
        vals = sb("vals", [P, QT, D])
        h = sb("h", [P, QT, D])
        hn = sb("hn", [P, QT, D])
        hT = sb("hT", [P, KC, S])
        bst = sb("bst", [P, QT, 6])
        mv = sb("mv", [P, QT, 2])
        rstd = sb("rstd", [P, QT])
        mhalf = sb("mhalf", [P, QT])
        hbias = sb("hbias", [P, 2, KC])
        qblk = sb("qblk", [P, KC, RQ, S])
        state = sb("state", [P, KC, 4, P])
        zc = sb("zc", [P, KC, B])
        gst = sb("gst", [P, KC, 2, 6])
        gmv = sb("gmv", [P, KC, 2])
        gmu = sb("gmu", [P, KC])
        gd = sb("gd", [P, KC])
        gvar = sb("gvar", [P, KC])
        grs = sb("grs", [P, KC])
        gscale = sb("gscale", [P, KC])
        gshift = sb("gshift", [P, KC])
        pA = sb("pA", [P, S], BF16)
        pB = sb("pB", [P, S], BF16)
        pr = sb("pr", [P, S])
        qT = pr
        hid = sb("hid", [P, FT, S])
        v1f = hid[:, 2:4, :].rearrange("p a b -> p (a b)")
        rqT, rkT = hid[:, 0:2, :], hid[:, 2:4, :]
        rv = hid[:, 4:6, :].rearrange("p a (c n) -> p (a c) n", n=D)
        ktok = hid[:, 6:8, :].rearrange("p a (c n) -> p (a c) n", n=D)
        amask = qkf[:, :, :].rearrange("p a (j n) -> p a j n", j=RQ)
        y = sb("y", [P, KC, S + 1])
        kvm = y[:, :, 0:3 * P].rearrange("p f (c n) -> p f c n", c=3)
        z = sb("z", [P, KC, S + 1])
        vT = z[:, :, 0:S]
        clsrow = sb("clsrow", [B, D])
        crow = sb("crow", [B, 4, D])
        cst = sb("cst", [B, 6])
        cmv = sb("cmv", [B, 4])
        cT = sb("cT", [P, 2, KC, B])
        one = sb("one", [P, 1])
        cP = sb("cP", [P, B])
        cA = sb("cA", [P, 2, B], BF16)
        chid = sb("chid", [P, FT, B])
        cQ = sb("cQ", [P, B])

        st_ps = ctx.enter_context(nc.psum_tensor("st_ps", [P, 2, S], F32))
        mx_ps = ctx.enter_context(nc.psum_tensor("mx_ps", [P, 2, S], F32))
        pv_ps = ctx.enter_context(nc.psum_tensor("pv_ps", [P, S], F32))
        ps = [ctx.enter_context(nc.psum_tensor(f"ps{i}", [P, S], F32)) for i in range(3)]

        front_in, rest_in, cls_in = sem("front_in"), sem("rest_in"), sem("cls_in")
        x_in = sem("x_in")
        full = [sem(f"full{i}") for i in range(3)]
        drained = [sem(f"drained{i}") for i in range(3)]
        max_full, max_done = sem("max_full"), sem("max_done")
        st_full, exp_done = sem("st_full"), sem("exp_done")
        pv_done, o_ready = sem("pv_done"), sem("o_ready")
        m_split, m_rows = sem("m_split"), sem("m_rows")
        qk_parts = sem("qk_parts")
        rep = [sem("rep0"), sem("rep1")]
        v_half = sem("v_half")
        ln_stats, ln_rstd, ln_done = sem("ln_stats"), sem("ln_rstd"), sem("ln_done")
        hb_done = sem("hb_done")
        qblk_in = sem("qblk_in")
        states = sem("states")
        y_chunk = sem("y_chunk")
        g_mean, g_dev, g_rstd, z_done, zc_done = sem("g_mean"), sem("g_dev"), sem("g_rstd"), sem("z_done"), sem("zc_done")
        p_rest, p_parts = sem("p_rest"), sem("p_parts")
        out_done = sem("out_done")
        consts, vconst = sem("consts"), sem("vconst")
        ones_done, zeros_done = sem("ones_done"), sem("zeros_done")
        c_hn, c_rstd, c_row, c_gelu, c_out, c_var = (sem("c_hn"), sem("c_rstd"), sem("c_row"), sem("c_gelu"),
                                                       sem("c_out"), sem("c_var"))
        c_cp = sem("c_cp")
        v_chain, p_chain = sem("v_chain"), sem("p_chain")

        def bank(key):
            return ps[use[key][0]]

        def wait_full(eng, key):
            i, n = use[key]
            eng.wait_ge(full[i], n + 1)

        def wait_drained(eng, key):
            i, n = use[key]
            eng.wait_ge(drained[i], n + 1)

        def wait_free(pe, key):
            i, n = use[key]
            if n:
                pe.wait_ge(drained[i], n)

        def inc_full(ins, key):
            ins.then_inc(full[use[key][0]], 1)

        def inc_drained(ins, key):
            ins.then_inc(drained[use[key][0]], 1)

        vcount, pcount = [0], [0]

        def vlink(ins):
            vcount[0] += 1
            ins.then_inc(v_chain, 1)
            nc.vector.wait_ge(v_chain, vcount[0])

        def plink(ins):
            pcount[0] += 1
            ins.then_inc(p_chain, 1)
            nc.gpsimd.wait_ge(p_chain, pcount[0])

        walk = [(it, t, STEPS * it + t, [(n, b) for u, n, b in stages(it) if u == t])
                for it in range(-1, B + 1) for t in range(STEPS)]
        block = ctx.enter_context(nc.Block())

        @block.sync
        def _(sp):
            sp.dma_start(fpack[:, :], front).then_inc(front_in, 16)
            sp.dma_start(xT[:, :, :], xt[0]).then_inc(x_in, 16)
            sp.dma_start(clsrow[:, :], cls).then_inc(cls_in, 16)
            sp.dma_start(rpack[:, :], rest).then_inc(rest_in, 16)
            sp.dma_start(v1f, v1).then_inc(rest_in, 16)
            for it, t, step, todo in walk:
                for half in range(2):
                    b = it + 1 - half
                    if not (t == (32 if half == 0 else 0) and 0 <= b < B):
                        continue
                    if b:
                        sp.wait_ge(st_full, STEPS * b - (STEPS // 2 if half == 0 else 0))
                    for i, (dst, part) in enumerate(((qr, Q_PART), (kr, K_PART))):
                        sp.wait_ge(qk_parts, 4 * b + 2 * half + i + 1)
                        for g in range(PARTS):
                            sp.dma_start(dst[HD * g:HD * (g + 1), HH * half:HH * (half + 1), :],
                                         split[:, i, part[g], half, :]).then_inc(rep[half], 16)
                for name, b in todo:
                    if name == "MT":
                        wait_drained(sp, (name, b))
                        if b >= NG:
                            sp.wait_ge(st_full, GS * (b - NG + 1))
                        g = b % NG
                        for i in range(2):
                            sp.dma_start(qr[KR + i:KR + i + 1, HG * g:HG * (g + 1), :],
                                         mrows[GS * i:GS * (i + 1), :]).then_inc(m_rows, 16)
                    if name == "FV1" and b + 1 < B:
                        wait_full(sp, (name, b))
                        sp.dma_start(xT[:, :, :], xt[b + 1]).then_inc(x_in, 16)
                    if name == "RQ1":
                        wait_drained(sp, ("RQ0", b))
                        wait_drained(sp, ("RQ1", b))
                        sp.wait_ge(zeros_done, 1)
                        if b:
                            wait_full(sp, ("A13", b - 1))
                        for j in range(RQ):
                            sp.dma_start(qblk[RD * j:RD * (j + 1), :, j, :],
                                         rqT[RD * j:RD * (j + 1), :, :]).then_inc(qblk_in, 16)
                    if name in ("V0", "V1"):
                        i = int(name[1])
                        wait_drained(sp, (name, b))
                        sp.dma_start(out[b, 1 + i * 2 * P:1 + (i + 1) * 2 * P, :].rearrange("(a p) n -> p a n", p=P),
                                     hn[:, 2 * i:2 * i + 2, :]).then_inc(out_done, 16)
                    if name == "CV":
                        sp.wait_ge(c_out, 1)
                        sp.dma_start(out[:, 0, :], crow[:, 2, :]).then_inc(out_done, 16)
            sp.wait_ge(out_done, 16 * (2 * B + 1))

        @block.tensor
        def _(pe):
            def mm(o, a, b, start, stop, check=False):
                return nc.tensor.matmul(o, a, b, start=start, stop=stop, skip_group_check=check)

            def tokens_out(key, lhs, weights, i):
                o = bank(key)
                for a in range(2):
                    for k in range(KC):
                        last = mm(o[:, a * D:(a + 1) * D], lhs[:, k, (2 * i + a) * P:(2 * i + a + 1) * P],
                                  weights[:, k, :], k == 0, k == KC - 1)
                inc_full(last, key)

            def features_out(key, weights, rhs, ft):
                o = bank(key)
                for k in range(KC):
                    last = mm(o[:, :], weights[:, k, ft * P:(ft + 1) * P], rhs[:, k, :], k == 0, k == KC - 1)
                inc_full(last, key)

            def transposes(keys, src, ready=None, before=0):
                for q in range(QT):
                    if ready:
                        pe.wait_ge(ready, before + q + 1)
                    for ft in range(KC):
                        if q == 0:
                            wait_free(pe, keys[ft])
                        last = nc.tensor.transpose(bank(keys[ft])[:, q * P:(q + 1) * P],
                                                   src[:, q, ft * P:(ft + 1) * P], ident)
                        if q == QT - 1:
                            inc_full(last, keys[ft])

            def stage(name, b):
                key = (name[:2], b) if name[0] == "Y" else (name, b)
                if name in ("VT1", "HT1", "HU1") or name in BESIDE:
                    return
                if name in ("VT0", "HT0", "HU0"):
                    keys = [(name[:2] + str(ft), b) for ft in range(KC)]
                    if name == "VT0":
                        wait_drained(pe, ("NR", NG * b + NG - 1))
                        transposes(keys, vals)
                    else:
                        transposes(keys, hn, ln_done, QT * (2 * b + (name == "HU0")))
                    return
                if name[0] != "Y" or name[2] == "0":
                    wait_free(pe, key)
                o = bank(key)
                if name == "MT":
                    pe.wait_ge(m_split, b + 1)
                    pe.wait_ge(consts, 3)
                    inc_full(nc.tensor.transpose(o[:, 0:P // 2].bitcast(BF16)[0:2 * GS, :],
                                                 mparts[:, :, :].rearrange("p a b -> p (a b)"), identb[:, :]), key)
                elif name == "NR":
                    pe.wait_ge(o_ready, b + 1)
                    for q in range(QT):
                        last = nc.tensor.transpose(o[:, q * P:(q + 1) * P], oT[:, q * P:(q + 1) * P], ident)
                    inc_full(last, key)
                elif name in ("FQ0", "FQ1", "FK0", "FK1"):
                    if name == "FQ0":
                        pe.wait_ge(front_in, 16)
                        pe.wait_ge(x_in, 16 * (b + 1))
                    features_out(key, wq if name[1] == "Q" else wk, xT, int(name[2]))
                elif name in ("FV0", "FV1"):
                    tokens_out(key, xT, wv, int(name[2]))
                elif name in ("OP0", "OP1"):
                    if name == "OP0":
                        pe.wait_ge(rest_in, 32)
                        wait_drained(pe, ("VT0", b))
                        wait_drained(pe, ("VT1", b))
                    tokens_out(key, vT, wout, int(name[2]))
                elif name in ("RQ0", "RQ1", "RK0", "RK1"):
                    if name == "RQ0":
                        wait_drained(pe, ("HT0", b))
                        wait_drained(pe, ("HT1", b))
                    features_out(key, rwq if name[1] == "Q" else rwk, hT, int(name[2]))
                elif name in ("RV0", "RV1"):
                    tokens_out(key, hT, rwv, int(name[2]))
                elif name in ("KT0", "KT1"):
                    if name == "KT0":
                        wait_drained(pe, ("RK0", b))
                        wait_drained(pe, ("RK1", b))
                    for a, c in enumerate(range(2) if name == "KT0" else range(2, 3)):
                        for ft in range(KC):
                            last = nc.tensor.transpose(o[:, a * D + ft * P:a * D + (ft + 1) * P],
                                                       rkT[:, ft, c * P:(c + 1) * P], ident)
                    inc_full(last, key)
                elif name in ("KV0", "KV1"):
                    ft = int(name[2])
                    if ft == 0:
                        for n in ("RV0", "RV1", "KT0", "KT1"):
                            wait_drained(pe, (n, b))
                    for c in range(3):
                        last = mm(o[:, c * P:(c + 1) * P], ktok[:, c, ft * P:(ft + 1) * P],
                                  rv[:, c, ft * P:(ft + 1) * P], True, True)
                    inc_full(last, key)
                elif name[0] == "A":
                    ft, c = int(name[1]), int(name[2])
                    if name == "A00":
                        pe.wait_ge(qblk_in, 64 * (b + 1))
                    inc_full(mm(o[:, :], rkT[:, ft, c * P:(c + 1) * P], qblk[:, ft, :, c * P:(c + 1) * P], True, True), key)
                elif name[0] == "Y":
                    ft, c = int(name[1]), int(name[2])
                    if name == "Y00":
                        pe.wait_ge(states, b + 1)
                    at = slice(c * P, (c + 1) * P)
                    mm(o[:, at], state[:, ft, c, :], rqT[:, ft, at], True, False, True)
                    wait_drained(pe, (f"A{ft}{c}", b))
                    for j in range(RQ):
                        last = mm(o[RD * j:RD * (j + 1), at], rv[:, c, ft * P + RD * j:ft * P + RD * (j + 1)],
                                  amask[:, c % 2, j, :], False, True, True)
                    if c == 3:
                        inc_full(last, key)
                    else:
                        last.then_inc(y_chunk, 1)
                elif name == "GM":
                    pe.wait_ge(g_mean, b + 1)
                    inc_full(mm(o[:, 0:KC], w("headmean"), gmv[:, :, 0], True, True), key)
                elif name == "GV":
                    pe.wait_ge(g_dev, b + 1)
                    inc_full(mm(o[:, 0:KC], w("headmean"), gd[:, :], True, True), key)
                elif name in ("WO0", "WO1"):
                    if name == "WO0":
                        pe.wait_ge(z_done, KC * (b + 1))
                    tokens_out(key, z, rwo, int(name[2]))
                elif name == "U1":
                    wait_drained(pe, ("HU0", b))
                    wait_drained(pe, ("HU1", b))
                    features_out(key, u1, hT, 0)
                elif name[0] == "H" and name[1].isdigit():
                    f = int(name[1])
                    if f == 0:
                        pe.wait_ge(p_parts, b + 1)
                        wait_drained(pe, ("U1", b))
                    at = slice(f * P, (f + 1) * P)
                    mm(o[:, :], v1p[:, 0, at], pA[:, :], True, False)
                    mm(o[:, :], v1p[:, 1, at], pA[:, :], False, False)
                    inc_full(mm(o[:, :], v1p[:, 2, at], pB[:, :], False, True), key)
                elif name == "U2":
                    for f in range(FT):
                        wait_drained(pe, (f"H{f}", b))
                        i = f % 2
                        last = mm(o[RANK * i:RANK * (i + 1), :], u2[:, f, :], hid[:, f, :], f < 2, f >= FT - 2, True)
                    inc_full(last, key)
                elif name in ("V0", "V1"):
                    i = int(name[1])
                    if i == 0:
                        wait_drained(pe, ("U2", b))
                    for a in range(2):
                        last = mm(o[:, a * D:(a + 1) * D], qT[:, (2 * i + a) * P:(2 * i + a + 1) * P], w("v2"), True, True)
                    inc_full(last, key)
                elif name == "C0":
                    pe.wait_ge(c_hn, 1)
                    for k in range(KC):
                        last = mm(o[:, k:k + 1], crow[0:1, 0, k * P:(k + 1) * P], one[0:1, :], True, True)
                    inc_full(last, key)
                elif name == "C1":
                    wait_drained(pe, ("C0", 0))
                    pe.wait_ge(rest_in, 32)
                    for ft in range(KC):
                        for k in range(KC):
                            last = mm(o[:, ft:ft + 1], rwq[:, k, ft * P:(ft + 1) * P], cT[:, 0, k, 0:1], k == 0, k == KC - 1)
                    inc_full(last, key)
                elif name == "C2":
                    for i, weights in enumerate((rwk, rwv)):
                        for k in range(KC):
                            last = mm(o[0:1, i * D:(i + 1) * D], cT[:, 0, k, 0:1], weights[:, k, :], k == 0, k == KC - 1)
                    inc_full(last, key)
                elif name == "C3":
                    wait_drained(pe, ("C2", 0))
                    for ft in range(KC):
                        at = slice(ft * P, (ft + 1) * P)
                        last = mm(o[:, at], crow[0:1, 1, at], crow[0:1, 2, at], True, True)
                    inc_full(last, key)
                elif name == "C4":
                    wait_drained(pe, ("C1", 0))
                    wait_drained(pe, ("C3", 0))
                    for ft in range(KC):
                        last = mm(o[:, ft:ft + 1], state[:, ft, 0, :], cT[:, 1, ft, 0:1], True, True)
                    inc_full(last, key)
                elif name == "CW":
                    pe.wait_ge(zc_done, B)
                    for k in range(KC):
                        last = mm(o[0:B, 0:D], zc[:, k, :], rwo[:, k, :], k == 0, k == KC - 1)
                    inc_full(last, key)
                elif name == "CT":
                    pe.wait_ge(c_hn, 2)
                    for k in range(KC):
                        last = mm(o[:, k * B:(k + 1) * B], crow[0:B, 0, k * P:(k + 1) * P], w("ident")[0:B, 0:B], True, True)
                    inc_full(last, key)
                elif name == "CU":
                    wait_drained(pe, ("CT", 0))
                    for k in range(KC):
                        last = mm(o[:, 0:B], u1[:, k, :], cT[:, 0, k, :], k == 0, k == KC - 1)
                    inc_full(last, key)
                elif name == "CH":
                    wait_drained(pe, ("CU", 0))
                    pe.wait_ge(c_cp, 1)
                    for f in range(FT):
                        at = slice(f * P, (f + 1) * P)
                        mm(o[:, f * B:(f + 1) * B], v1p[:, 0, at], cA[:, 0, :], True, False)
                        mm(o[:, f * B:(f + 1) * B], v1p[:, 1, at], cA[:, 0, :], False, False)
                        last = mm(o[:, f * B:(f + 1) * B], v1p[:, 2, at], cA[:, 1, :], False, True)
                    inc_full(last, key)
                elif name == "CQ":
                    pe.wait_ge(c_gelu, 1)
                    for f in range(FT):
                        i = f % 2
                        last = mm(o[RANK * i:RANK * (i + 1), 0:B], u2[:, f, :], chid[:, f, :], f < 2, f >= FT - 2, True)
                    inc_full(last, key)
                elif name == "CV":
                    wait_drained(pe, ("CQ", 0))
                    inc_full(mm(o[0:B, 0:D], cQ[:, :], w("v2"), True, True), key)
                else:
                    raise ValueError(name)

            for it, t, step, todo in walk:
                m = step + AHEAD
                if 0 <= m < B * STEPS:
                    head, q = m % STEPS // QT, m % QT
                    if m % STEPS in (0, STEPS // 2):
                        pe.wait_ge(rep[m % STEPS // (STEPS // 2)], 16 * 2 * PARTS * (m // STEPS + 1))
                    if m >= 2:
                        pe.wait_ge(max_done, m - 1)
                    mm(mx_ps[:, m % 2, :], qr[0:KR, head, q * P:(q + 1) * P], kr[0:KR, head, :], True, True)\
                        .then_inc(max_full, 1)
                if 0 <= step < B * STEPS:
                    n, kt, j = step // GS, step % GS // HG, step % HG
                    head = HG * (n % NG) + j
                    if step % GS == 0:
                        pe.wait_ge(m_rows, 32 * (n + 1))
                        pe.wait_ge(ones_done, 1)
                    if step >= 2:
                        pe.wait_ge(exp_done, step - 1)
                    mm(st_ps[:, step % 2, :], kr[:, head, kt * P:(kt + 1) * P], qr[:, head, :], True, True)\
                        .then_inc(st_full, 1)
                last_exp = step - PV_LAG
                if 0 <= last_exp < B * STEPS and last_exp % HG == HG - 1:
                    n, kt = last_exp // GS, last_exp % GS // HG
                    pe.wait_ge(exp_done, last_exp + 1)
                    if kt == 0 and n % (NG // 2) == 0:
                        pe.wait_ge(v_half, n // (NG // 2) + 1)
                    if kt == 0 and n:
                        pe.wait_ge(o_ready, n)
                    for j in range(HG):
                        last = mm(pv_ps[32 * j:32 * (j + 1), :], vaug[:, kt, HG * (n % NG) + j, :], probs[:, kt, j, :],
                                  kt == 0, kt == QT - 1)
                    last.then_inc(pv_done, 1)
                for name, b in todo:
                    stage(name, b)

        @block.scalar
        def _(act):
            def stage(name, b):
                key = (name, b)
                if name in ("FQ0", "FQ1", "FK0", "FK1"):
                    wait_full(act, key)
                    i, half = int(name[1] == "K"), int(name[2])
                    if 4 * b + 2 * half:
                        act.wait_ge(qk_parts, 4 * b + 2 * half - 1 + i)
                    if name == "FQ0" and b == 0:
                        act.wait_ge(consts, 3)
                    inc_drained(nc.scalar.activation(qkf[:, i, :], bank(key)[:, :], ACT.Identity,
                                                     bias=hbias[:, i, half:half + 1], scale=0.5), key)
                elif name in ("VT0", "VT1"):
                    wait_full(act, key)
                    if b:
                        wait_full(act, ("OP1", b - 1))
                    inc_drained(nc.scalar.copy(vT[:, int(name[2]), :], bank(key)[:, :]), key)
                elif name in ("HT0", "HU0"):
                    wait_full(act, key)
                    if name[1] == "U":
                        wait_full(act, ("RV1", b))
                    elif b:
                        wait_full(act, ("U1", b - 1))
                    inc_drained(nc.scalar.copy(hT[:, int(name[2]), :], bank(key)[:, :]), key)
                elif name in ("RV0", "RV1"):
                    wait_full(act, key)
                    if b:
                        wait_full(act, ("Y1", b - 1))
                    i = int(name[2])
                    inc_drained(nc.scalar.copy(rv[:, 2 * i:2 * i + 2, :].rearrange("p a b -> p (a b)"), bank(key)[:, :]), key)
                elif name in ("KT0", "KT1"):
                    wait_full(act, key)
                    if b:
                        wait_full(act, ("KV1", b - 1))
                    c, n = (0, 2) if name == "KT0" else (2, 1)
                    inc_drained(nc.scalar.copy(ktok[:, c:c + n, :].rearrange("p a b -> p (a b)"), bank(key)[:, 0:n * D]), key)
                elif name in ("Y03", "Y13"):
                    ft = int(name[1])
                    wait_full(act, (name[:2], b))
                    if b:
                        act.wait_ge(z_done, KC * b)
                        act.wait_ge(g_mean, b)
                    inc_drained(nc.scalar.copy(y[:, ft, 0:S], bank((name[:2], b))[:, :]), (name[:2], b))
                elif name[0] == "H" and name[1].isdigit():
                    f = int(name[1])
                    wait_full(act, key)
                    inc_drained(nc.scalar.activation(hid[:, f, :], bank(key)[:, :], ACT.Gelu_apprx_tanh,
                                                     bias=w("b1")[:, f:f + 1]), key)
                elif name == "U2":
                    wait_full(act, key)
                    if b:
                        wait_full(act, ("V1", b - 1))
                    inc_drained(nc.scalar.copy(qT[:, :], bank(key)[:, :]), key)
                elif name == "CH":
                    wait_drained(act, key)
                    nc.scalar.activation(chid[:, :, :], chid[:, :, :], ACT.Gelu_apprx_tanh).then_inc(c_gelu, 1)

            for it, t, step, todo in walk:
                if 0 <= step < B * STEPS:
                    n, kt, j = step // GS, step % GS // HG, step % HG
                    act.wait_ge(st_full, step + 1)
                    if n and j == 0:
                        act.wait_ge(pv_done, QT * (n - 1) + kt + 1)
                    nc.scalar.activation(probs[:, kt, j, :], st_ps[:, step % 2, :], ACT.Exp).then_inc(exp_done, 1)
                n = (step - PV_LAG) // GS
                if 0 <= n < B * NG and (step - PV_LAG) % GS == GS - 1:
                    act.wait_ge(pv_done, QT * (n + 1))
                    if n:
                        wait_full(act, ("NR", n - 1))
                    nc.scalar.copy(oT[:, :], pv_ps[:, :]).then_inc(o_ready, 1)
                for name, b in todo:
                    stage(name, b)

        @block.vector
        def _(dve):
            dve.wait_ge(front_in, 16)
            nc.vector.tensor_copy(identb[:, :], ident).then_inc(consts, 1)
            for i, name in enumerate(("qbias", "kbias")):
                nc.vector.tensor_scalar(hbias[:, i, :], w(name), 0.5, None, ALU.mult).then_inc(consts, 1)
            def row_stats(src, n):
                vlink(nc.vector.bn_stats(cst[0:n, :], src))
                vlink(nc.vector.bn_aggr(cmv[0:n, 0:2], cst[0:n, :]))
                nc.vector.tensor_scalar(cmv[0:n, 2:3], cmv[0:n, 1:2], EPS, None, ALU.add).then_inc(c_var, 1)

            def row_norm(src, n, count):
                dve.wait_ge(c_rstd, count)
                nc.vector.tensor_scalar(crow[0:n, 0, :], src, cmv[0:n, 0:1], cmv[0:n, 3:4],
                                        ALU.subtract, ALU.mult).then_inc(c_hn, 1)

            def class_norm():
                dve.wait_ge(cls_in, 16)
                row_stats(clsrow[0:1, :], 1)
                row_norm(clsrow[0:1, :], 1, 1)

            def v1_parts():
                rest_of_v1 = hid[:, 4:6, :].rearrange("p a b -> p (a b)")
                dve.wait_ge(rest_in, 32)
                vlink(nc.vector.tensor_copy(v1p[:, 0, :], v1f))
                vlink(nc.vector.tensor_tensor(rest_of_v1, v1f, v1p[:, 0, :], ALU.subtract))
                vlink(nc.vector.tensor_copy(v1p[:, 1, :], rest_of_v1))
                vlink(nc.vector.tensor_tensor(v1p[0:64, 2, :], rest_of_v1[0:64, :], v1p[0:64, 1, :], ALU.subtract))
                vlink(nc.vector.tensor_copy(v1p[64:128, 2, :], v1p[64:128, 0, :]))

            def layer_norm_stats(key, i):
                wait_drained(dve, key)
                for q in (2 * i, 2 * i + 1):
                    nc.vector.bn_stats(bst[:, q, :], h[:, q, :]).then_inc(v_chain, 1)
                vcount[0] += 2
                dve.wait_ge(v_chain, vcount[0])
                for q in (2 * i, 2 * i + 1):
                    nc.vector.bn_aggr(mv[:, q, :], bst[:, q, :]).then_inc(v_chain, 1)
                vcount[0] += 2
                dve.wait_ge(v_chain, vcount[0])
                nc.vector.tensor_scalar(rstd[:, 2 * i:2 * i + 2], mv[:, 2 * i:2 * i + 2, 1], EPS, None,
                                        ALU.add).then_inc(ln_stats, 1)

            def layer_norm(n, i):
                dve.wait_ge(ln_rstd, 2 * n + i + 1)
                for q in (2 * i, 2 * i + 1):
                    nc.vector.tensor_scalar(hn[:, q, :], h[:, q, :], mv[:, q, 0:1], rstd[:, q:q + 1],
                                            ALU.subtract, ALU.mult).then_inc(ln_done, 1)

            def stage(name, b):
                key = (name, b)
                if name in ("SQ0", "SK0", "SQ1", "SK1"):
                    i, half = int(name[1] == "K"), int(name[2])
                    wait_drained(dve, ("F" + name[1:], b))
                    if b:
                        dve.wait_ge(rep[half], 16 * 2 * PARTS * b)
                    vlink(nc.vector.tensor_copy(split[:, i, 0, half, :], qkf[:, i, :]))
                    vlink(nc.vector.tensor_tensor(qkf[:, i, :], qkf[:, i, :], split[:, i, 0, half, :], ALU.subtract))
                    vlink(nc.vector.tensor_copy(split[:, i, 1, half, :], qkf[:, i, :]))
                    nc.vector.tensor_tensor(split[:, i, 2, half, :], qkf[:, i, :], split[:, i, 1, half, :],
                                            ALU.subtract).then_inc(qk_parts, 1)
                elif name in ("FV0", "FV1"):
                    wait_full(dve, key)
                    if b:
                        dve.wait_ge(v_half, 2 * b)
                    i = int(name[2])
                    vb = repeat(w("vbias").rearrange("p (a n) -> p a n", a=1), 1, 2)
                    inc_drained(nc.vector.tensor_tensor(vstage[:, 2 * i:2 * i + 2, :],
                                                        bank(key)[:, :].rearrange("p (a n) -> p a n", a=2), vb, ALU.add), key)
                elif name == "MT":
                    wait_full(dve, key)
                    if b:
                        dve.wait_ge(m_rows, 32 * b)
                    inc_drained(nc.vector.tensor_copy(mrows[:, :], bank(key)[:, 0:P // 2].bitcast(BF16)[0:2 * GS, :]), key)
                elif name == "NR":
                    wait_full(dve, key)
                    g = b % NG
                    if b:
                        wait_drained(dve, ("NR", b - 1))
                    if g == 0 and b:
                        wait_full(dve, ("VT1", b // NG - 1))
                    o = bank(key)[:, :].rearrange("p (q j c) -> p q j c", q=QT, j=HG)
                    vlink(nc.vector.reciprocal(rsum[:, :, :], o[:, :, :, HD]))
                    r = repeat(rsum[:, :, :].rearrange("p q (j a) -> p q j a", a=1), 3, HD)
                    dst = vals[:, :, HG * HD * g:HG * HD * (g + 1)].rearrange("p q (j c) -> p q j c", j=HG)
                    inc_drained(nc.vector.tensor_tensor(dst, o[:, :, :, 0:HD], r, ALU.mult), key)
                elif name in ("OP0", "OP1"):
                    wait_full(dve, key)
                    i = int(name[2])
                    if b:
                        wait_drained(dve, ("V1", b - 1))
                        wait_drained(dve, ("V0", b - 1))
                    bb = repeat(w("bout").rearrange("p (a n) -> p a n", a=1), 1, 2)
                    inc_drained(nc.vector.tensor_tensor(h[:, 2 * i:2 * i + 2, :],
                                                        bank(key)[:, :].rearrange("p (a n) -> p a n", a=2), bb, ALU.add), key)
                    if b:
                        dve.wait_ge(ln_done, QT * 2 * b)
                    layer_norm_stats(key, i)
                elif name == "LA":
                    if b:
                        dve.wait_ge(out_done, 32 * b)
                    layer_norm(2 * b, 0)
                    layer_norm(2 * b, 1)
                elif name in ("HT1", "HU1"):
                    wait_full(dve, key)
                    if name[1] == "U":
                        wait_full(dve, ("RV1", b))
                    elif b:
                        wait_full(dve, ("U1", b - 1))
                    inc_drained(nc.vector.tensor_copy(hT[:, 1, :], bank(key)[:, :]), key)
                elif name in ("RQ0", "RQ1", "RK0", "RK1"):
                    wait_full(dve, key)
                    ft = int(name[2])
                    if b:
                        wait_full(dve, ("Y1", b - 1))
                        dve.wait_ge(qblk_in, 64 * b)
                        if name[1] == "K":
                            wait_full(dve, ("A13", b - 1))
                    table, dst = (gq, rqT) if name[1] == "Q" else (gk, rkT)
                    inc_drained(nc.vector.tensor_tensor(dst[:, ft, :], bank(key)[:, :], table[:, ft, :], ALU.mult), key)
                elif name in ("KV0", "KV1"):
                    wait_full(dve, key)
                    if b:
                        dve.wait_ge(states, b)
                    ft = int(name[2])
                    mask = repeat(w("blocks").rearrange("p (a n) -> p a n", a=1), 1, 3)
                    inc_drained(nc.vector.tensor_tensor(kvm[:, ft, :, :],
                                                        bank(key)[:, 0:3 * P].rearrange("p (a n) -> p a n", a=3),
                                                        mask, ALU.mult), key)
                elif name == "SS":
                    for n in ("KV0", "KV1"):
                        wait_drained(dve, (n, b))
                    if b:
                        wait_full(dve, ("Y1", b - 1))
                    else:
                        wait_drained(dve, ("C3", 0))
                    for c in range(3):
                        ins = nc.vector.tensor_tensor(state[:, :, c + 1, :], state[:, :, c, :], kvm[:, :, c, :], ALU.add)
                        if c < 2:
                            vlink(ins)
                        else:
                            ins.then_inc(states, 1)
                elif name[0] == "A":
                    ft, c = int(name[1]), int(name[2])
                    wait_full(dve, key)
                    if c >= 2:
                        dve.wait_ge(y_chunk, 3 * (2 * b + ft) + c - 1)
                    elif ft:
                        wait_full(dve, ("Y0", b))
                    else:
                        dve.wait_ge(qk_parts, 4 * min(b + 3, B))
                        if b:
                            wait_full(dve, ("Y1", b - 1))
                    mask = repeat(w("causal").rearrange("p (a n) -> p a n", a=1), 1, RQ)
                    inc_drained(nc.vector.tensor_tensor(amask[:, c % 2, :, :],
                                                        bank(key)[:, :].rearrange("p (a n) -> p a n", a=RQ),
                                                        mask, ALU.mult), key)
                elif name in ("Y03", "Y13"):
                    ft = int(name[1])
                    wait_drained(dve, (name[:2], b))
                    if b == 0 and ft == 0:
                        wait_drained(dve, ("C4", 0))
                    if b:
                        dve.wait_ge(g_dev, b)
                    half = (S + 2) // 2
                    nc.vector.bn_stats(gst[:, ft, 0, :], y[:, ft, 0:half]).then_inc(v_chain, 1)
                    nc.vector.bn_stats(gst[:, ft, 1, :], y[:, ft, half:S + 1]).then_inc(v_chain, 1)
                    vcount[0] += 2
                    dve.wait_ge(v_chain, vcount[0])
                    last = nc.vector.bn_aggr(gmv[:, ft, :], gst[:, ft, :, :].rearrange("p a b -> p (a b)"))
                    if ft:
                        last.then_inc(g_mean, 1)
                    else:
                        vlink(last)
                elif name == "GM":
                    wait_full(dve, key)
                    dve.wait_ge(g_mean, b + 1)
                    if b:
                        dve.wait_ge(z_done, KC * b)
                        wait_full(dve, ("GV", b - 1))
                    inc_drained(nc.vector.tensor_copy(gmu[:, :], bank(key)[:, 0:KC]), key)
                    wait_drained(dve, key)
                    vlink(nc.vector.tensor_tensor(gvar[:, :], gmv[:, :, 0], gmu[:, :], ALU.subtract))
                    vlink(nc.vector.tensor_tensor(gvar[:, :], gvar[:, :], gvar[:, :], ALU.mult))
                    nc.vector.tensor_tensor(gd[:, :], gvar[:, :], gmv[:, :, 1], ALU.add).then_inc(g_dev, 1)
                elif name == "GV":
                    wait_full(dve, key)
                    dve.wait_ge(g_dev, b + 1)
                    inc_drained(nc.vector.tensor_scalar(gvar[:, :], bank(key)[:, 0:KC], EPS, None, ALU.add), key)
                elif name == "GZ":
                    dve.wait_ge(g_rstd, b + 1)
                    vlink(nc.vector.tensor_tensor(gscale[:, :], grs[:, :], w("gnw"), ALU.mult))
                    vlink(nc.vector.tensor_tensor(gmu[:, :], gmu[:, :], gscale[:, :], ALU.mult))
                    vlink(nc.vector.tensor_tensor(gshift[:, :], w("gnb"), gmu[:, :], ALU.subtract))
                    if b:
                        wait_full(dve, ("WO1", b - 1))
                        dve.wait_ge(zc_done, b)
                    for ft in range(KC):
                        nc.vector.tensor_scalar(z[:, ft, :], y[:, ft, :], gscale[:, ft:ft + 1], gshift[:, ft:ft + 1],
                                                ALU.mult, ALU.add).then_inc(z_done, 1)
                elif name in ("WO0", "WO1"):
                    wait_full(dve, key)
                    dve.wait_ge(ln_done, QT * (2 * b + 1))
                    i = int(name[2])
                    hv = h[:, 2 * i:2 * i + 2, :].rearrange("p a b -> p (a b)")
                    inc_drained(nc.vector.tensor_tensor(hv, bank(key)[:, :], hv, ALU.add), key)
                    layer_norm_stats(key, i)
                elif name == "LB":
                    wait_full(dve, ("HT1", b))
                    layer_norm(2 * b + 1, 0)
                    layer_norm(2 * b + 1, 1)
                elif name == "U1":
                    wait_full(dve, key)
                    if b:
                        wait_full(dve, ("H7", b - 1))
                        dve.wait_ge(p_parts, b)
                    up = slice(P // 2, P)
                    vlink(nc.vector.tensor_copy(pA[:, :], bank(key)[:, :]))
                    inc_drained(nc.vector.tensor_tensor(pr[up, :], bank(key)[up, :], pA[up, :], ALU.subtract), key)
                    wait_drained(dve, key)
                    vlink(nc.vector.tensor_copy(pA[up, :], pr[up, :]))
                    vlink(nc.vector.tensor_tensor(pB[up, :], pr[up, :], pA[up, :], ALU.subtract))
                    nc.vector.tensor_copy(pB[0:P // 2, :], pA[0:P // 2, :]).then_inc(p_parts, 1)
                elif name in ("V0", "V1"):
                    wait_full(dve, key)
                    dve.wait_ge(hb_done, b + 1)
                    wait_full(dve, ("HU1", b))
                    i = int(name[1])
                    inc_drained(nc.vector.tensor_tensor(hn[:, 2 * i:2 * i + 2, :].rearrange("p a b -> p (a b)"),
                                                        bank(key)[:, :], h[:, 2 * i:2 * i + 2, :].rearrange("p a b -> p (a b)"),
                                                        ALU.add), key)
                elif name == "C0":
                    wait_full(dve, key)
                    inc_drained(nc.vector.tensor_copy(cT[:, 0, :, 0], bank(key)[:, 0:KC]), key)
                elif name == "C1":
                    wait_full(dve, key)
                    inc_drained(nc.vector.tensor_copy(cT[:, 1, :, 0], bank(key)[:, 0:KC]), key)
                elif name == "C2":
                    wait_full(dve, key)
                    inc_drained(nc.vector.tensor_copy(crow[0:1, 1:3, :].rearrange("p a b -> p (a b)"), bank(key)[0:1, :]), key)
                elif name == "C3":
                    wait_full(dve, key)
                    mask = repeat(w("blocks").rearrange("p (a n) -> p a n", a=1), 1, KC)
                    inc_drained(nc.vector.tensor_tensor(state[:, :, 0, :],
                                                        bank(key)[:, 0:KC * P].rearrange("p (a n) -> p a n", a=KC),
                                                        mask, ALU.mult), key)
                elif name == "C4":
                    wait_full(dve, key)
                    inc_drained(nc.vector.tensor_copy(y[:, :, S], bank(key)[:, 0:KC]), key)
                elif name == "CW":
                    wait_full(dve, key)
                    wait_full(dve, ("C0", 0))
                    inc_drained(nc.vector.tensor_tensor(crow[:, 3, :], bank(key)[0:B, 0:D], clsrow[:, :], ALU.add), key)
                    wait_drained(dve, key)
                    dve.wait_ge(c_hn, 1)
                    row_stats(crow[:, 3, :], B)
                    row_norm(crow[:, 3, :], B, 2)
                elif name == "CT":
                    wait_full(dve, key)
                    wait_full(dve, ("C2", 0))
                    inc_drained(nc.vector.tensor_copy(cT[:, 0, :, :].rearrange("p a b -> p (a b)"), bank(key)[:, 0:KC * B]), key)
                elif name == "CU":
                    wait_full(dve, key)
                    vlink(nc.vector.tensor_copy(cA[:, 0, :], bank(key)[:, 0:B]))
                    vlink(nc.vector.tensor_copy(cA[0:64, 1, :], cA[0:64, 0, :]))
                    inc_drained(nc.vector.tensor_tensor(cP[:, :], bank(key)[:, 0:B], cA[:, 0, :], ALU.subtract), key)
                    wait_drained(dve, key)
                    vlink(nc.vector.tensor_copy(cA[64:128, 0, :], cP[64:128, :]))
                    nc.vector.tensor_tensor(cA[64:128, 1, :], cP[64:128, :], cA[64:128, 0, :], ALU.subtract).then_inc(c_cp, 1)
                elif name == "CH":
                    wait_full(dve, key)
                    bb = repeat(w("b1").rearrange("p (f a) -> p f a", a=1), 2, B)
                    inc_drained(nc.vector.tensor_tensor(chid[:, :, :], bank(key)[:, 0:FT * B].rearrange("p (f a) -> p f a", a=B),
                                                        bb, ALU.add), key)
                elif name == "CQ":
                    wait_full(dve, key)
                    inc_drained(nc.vector.tensor_copy(cQ[:, :], bank(key)[:, 0:B]), key)
                elif name == "CV":
                    wait_full(dve, key)
                    vlink(nc.vector.tensor_tensor(crow[:, 1, :], bank(key)[0:B, 0:D], crow[:, 3, :], ALU.add))
                    nc.vector.tensor_tensor(crow[:, 2, :], crow[:, 1, :], w("b2")[0:B, :], ALU.add).then_inc(c_out, 1)

            for it, t, step, todo in walk:
                m = step + AHEAD
                if 0 <= m < B * STEPS:
                    n = m // GS
                    dve.wait_ge(max_full, m + 1)
                    if n >= 2 and m % GS == 0:
                        dve.wait_ge(m_split, n - 1)
                    nc.vector.tensor_reduce(negmax[:, n % 2, m % GS:m % GS + 1], mx_ps[:, m % 2, :], AX, ALU.max,
                                            negate=True).then_inc(max_done, 1)
                    if m % GS == GS - 1:
                        dve.wait_ge(max_done, m + 1)
                        if n:
                            wait_full(dve, ("MT", n - 1))
                        vlink(nc.vector.tensor_copy(mparts[:, 0, :], negmax[:, n % 2, :]))
                        nc.vector.tensor_tensor(mparts[:, 1, :], negmax[:, n % 2, :], mparts[:, 0, :],
                                                ALU.subtract).then_inc(m_split, 1)
                if step == 25:
                    class_norm()
                if step == 50:
                    v1_parts()
                for name, b in todo:
                    stage(name, b)

        @block.gpsimd
        def _(pool):
            nc.gpsimd.memset(kr[KR:KM, :, :], 1.0).then_inc(ones_done, 1)
            pool.wait_ge(ones_done, 1)
            nc.gpsimd.memset(mhalf[:, :], -0.5).then_inc(p_chain, 1)
            nc.gpsimd.memset(one[:, :], 1.0).then_inc(p_chain, 1)
            pcount[0] += 2
            nc.gpsimd.memset(vaug[:, :, :, HD:32], 0.0).then_inc(vconst, 1)
            pool.wait_ge(vconst, 1)
            nc.gpsimd.memset(vaug[:, :, :, HD:HD + 1], 1.0).then_inc(vconst, 1)
            nc.gpsimd.memset(qblk[:, :, :, :], 0.0).then_inc(zeros_done, 1)

            def class_rstd(n, count):
                pool.wait_ge(c_var, count)
                pool.wait_ge(p_chain, 2)
                nc.gpsimd.tensor_tensor(cmv[0:n, 3:4], cmv[0:n, 2:3], mhalf[0:n, 0:1], ALU.pow).then_inc(c_rstd, 1)

            def layer_norm_rstd(n, i):
                pool.wait_ge(ln_stats, 2 * n + i + 1)
                at = slice(2 * i, 2 * i + 2)
                nc.gpsimd.tensor_tensor(rstd[:, at], rstd[:, at], mhalf[:, at], ALU.pow).then_inc(ln_rstd, 1)

            for it, t, step, todo in walk:
                if step == 25:
                    class_rstd(1, 1)
                for half in range(2):
                    b = it + 1 - half
                    if t == (40 if half == 0 else 4) and 0 <= b < B:
                        wait_drained(pool, ("FV0", b))
                        wait_drained(pool, ("FV1", b))
                        pool.wait_ge(vconst, 2)
                        if b:
                            pool.wait_ge(pv_done, QT * (NG * b - (NG // 2 if half == 0 else 0)))
                        heads = slice(HH * half, HH * (half + 1))
                        nc.gpsimd.tensor_scalar(vaug[:, :, heads, 0:HD],
                                                vstage[:, :, HH * HD * half:HH * HD * (half + 1)]
                                                .rearrange("p q (h d) -> p q h d", d=HD), 1.0, None, ALU.mult)\
                            .then_inc(v_half, 1)
                for name, b in todo:
                    if name in ("OP0", "OP1"):
                        layer_norm_rstd(2 * b, int(name[2]))
                    elif name == "GV":
                        wait_drained(pool, ("GV", b))
                        if b:
                            pool.wait_ge(z_done, KC * b)
                        nc.gpsimd.tensor_tensor(grs[:, :], gvar[:, :], mhalf[:, 0:KC], ALU.pow).then_inc(g_rstd, 1)
                        pool.wait_ge(z_done, KC * (b + 1))
                        nc.gpsimd.tensor_scalar(zc[:, :, b], z[:, :, S], 1.0, None, ALU.mult).then_inc(zc_done, 1)
                    elif name == "WO0":
                        layer_norm_rstd(2 * b + 1, 0)
                    elif name == "WO1":
                        layer_norm_rstd(2 * b + 1, 1)
                        pool.wait_ge(ln_done, QT * (2 * b + 2))
                        bb = repeat(w("b2").rearrange("p (a n) -> p a n", a=1), 1, QT)
                        nc.gpsimd.tensor_tensor(h[:, :, :], h[:, :, :], bb, ALU.add).then_inc(hb_done, 1)
                    elif name == "CW":
                        class_rstd(B, 2)


def kernel(**inputs):
    import numpy as np
    import concourse.bacc as bacc
    from concourse.bass_utils import run_bass_kernel_spmd as run

    a = {k: np.asarray(v) for k, v in inputs.items()}
    f32 = np.float32

    def tiles(m):
        return np.ascontiguousarray(m.reshape(-1, P, m.shape[1]).transpose(1, 0, 2)).reshape(P, -1)

    def column(v):
        return np.ascontiguousarray(v.reshape(-1, P).T)

    def everywhere(v):
        return np.broadcast_to(v, (P, v.size))

    wqkv = a["L0_tok_w_qkv"].reshape(2, HH, 3, HD, D)
    bqkv = a["L0_tok_b_qkv"].reshape(2, HH, 3, HD)
    pick = lambda i: (wqkv[:, :, i].transpose(0, 2, 1, 3).reshape(D, D).T, bqkv[:, :, i].transpose(0, 2, 1).reshape(D))
    (wq, bq), (wk, bk) = pick(0), pick(1)
    wv, bv = wqkv[:, :, 2].reshape(D, D).T, bqkv[:, :, 2].reshape(D)
    v = {
        "wq": tiles(wq), "wk": tiles(wk), "wv": tiles(wv), "qbias": column(bq), "kbias": column(bk),
        "vbias": everywhere(bv), "ident": np.eye(P, dtype=f32),
        "wout": tiles(a["L0_tok_w_out"].T), "bout": everywhere(a["L0_tok_b_out"]),
        "rwq": tiles(a["L0_attn_Wq"].T), "rwk": tiles(a["L0_attn_Wk"].T), "rwv": tiles(a["L0_attn_Wv"].T),
        "rwo": tiles(a["L0_attn_Wo"].T), "gnw": column(a["L0_attn_gn_weight"]), "gnb": column(a["L0_attn_gn_bias"]),
        "u1": tiles(np.concatenate([a["L0_ffn_U1"]] * 2, axis=1)), "b1": column(a["L0_ffn_b1"]), "u2": tiles(a["L0_ffn_U2"]), "v2": np.concatenate([a["L0_ffn_V2"]] * 2),
        "b2": everywhere(a["L0_ffn_b2"]),
    }
    decay = (f32(1) - np.exp(np.linspace(np.log(1 / 32), np.log(1 / 512), RH).astype(f32))).astype(np.float64)
    pos = np.arange(1, S + 1)
    power = np.repeat(decay, RD)[:, None] ** pos[None]
    v["gq"], v["gk"] = tiles(power.astype(f32)), tiles((1 / power).astype(f32))
    i = np.arange(P)
    v["causal"] = (i[:, None] <= i[None]).astype(f32)
    v["blocks"] = (i[:, None] // RD == i[None] // RD).astype(f32)
    v["headmean"] = v["blocks"] * f32(1 / RD)
    arrays = {
        "xt": np.ascontiguousarray(a["x"].reshape(B, S, KC, P).transpose(0, 3, 2, 1)),
        "front": np.concatenate([v[n] for n, _ in FRONT], axis=1),
        "rest": np.concatenate([v[n] for n, _ in REST], axis=1),
        "v1": np.concatenate([a["L0_ffn_V1"]] * 2),
        "cls": np.ascontiguousarray(np.broadcast_to(a["cls_tok"].reshape(1, D), (B, D))),
    }
    nc = bacc.Bacc("TRN2", target_bir_lowering=False, num_devices=1)
    args = [nc.dram_tensor(n, m.shape, mybir.dt.from_np(m.dtype), kind="ExternalInput").ap() for n, m in arrays.items()]
    out = nc.dram_tensor("out_0_dram", (B, S + 1, D), F32, kind="ExternalOutput").ap()
    vit_tower(nc, *args, out)
    return run(nc, [arrays], core_ids=[0]).results[0]["out_0_dram"]
```

```python
from collections import namedtuple
from contextlib import ExitStack

import concourse.bass as bass
from concourse import mybir

ALU = mybir.AluOpType
ACT = mybir.ActivationFunctionType
F32 = mybir.dt.float32
BF16 = mybir.dt.bfloat16
F32R = mybir.dt.float32r
AX = mybir.AxisListType.X

B, S, D = 4, 512, 256
P = 128
QT = S // P
KC = D // P
NH, HD = 16, 16
HG = 4
NG = NH // HG
STEPS = NH * QT
GS = HG * QT
HH = NH // 2
PARTS = 6
KR = PARTS * HD
KM = KR + 2
Q_PART = [0, 0, 1, 1, 0, 2]
K_PART = [0, 1, 0, 1, 2, 0]
RH, RD = 8, 32
RQ = 4
RANK, FF = 64, 1024
FT = FF // P
EPS = 1e-5
AHEAD = 23
PV_LAG = 3

FRONT = [("qbias", KC), ("kbias", KC), ("vbias", D), ("ident", P)]
REST = [("bout", D), ("gq", KC * P), ("gk", KC * P), ("gchunk", KC), ("gblocks", KC * P), ("causal", P), ("blocks", P),
        ("headmean", P), ("gnw", KC), ("gnb", KC), ("b1", FT), ("u2", FT * RANK), ("v2", D), ("b2", D)]
FRONT_WEIGHTS = [("wq", KC * D), ("wk", KC * D), ("wv", KC * D)]
WEIGHTS = FRONT_WEIGHTS + [("wout", KC * D), ("rwq", KC * D), ("rwk", KC * D), ("rwv", KC * D), ("rwo", KC * D),
                           ("u1", KC * P), ("v1", FF)]

AT = {
    "FQ0": 7, "FK0": 11, "FQ1": 14, "FK1": 14, "FV0": 28, "FV1": 28, "VT": 5, "OP0": 8, "OP1": 8, "HT": 12,
    "RQ0": 14, "RQ1": 14, "RK0": 16, "RK1": 18, "RV0": 17, "RV1": 19, "KT0": 20, "KT1": 22, "KV0": 24, "KV1": 24,
    "A00": 27, "A01": 27, "Y00": 28, "A02": 28, "Y01": 28, "A03": 28, "Y02": 29, "A10": 31, "Y03": 31, "A11": 31,
    "Y10": 31, "A12": 31, "Y11": 31, "A13": 31, "Y12": 33, "Y13": 33, "GM": 35, "GV": 37, "WO0": 40, "WO1": 40,
    "HU": 45, "U1": 48, "H0": 53, "H1": 53, "H2": 53, "Q0": 53, "H3": 53, "Q1": 53, "H4": 53, "Q2": 53, "H5": 53,
    "Q3": 53, "H6": 53, "Q4": 53, "H7": 53, "Q5": 53, "Q6": 53, "Q7": 54, "V0": 56, "V1": 60, "SQ0": 10, "SK0": 12,
    "SQ1": 17, "SK1": 19, "LA": 11, "SS": 25, "GZ": 38, "LB": 43, "XS": 4,
}
BESIDE = ("XS", "SQ0", "SK0", "SQ1", "SK1", "LA", "SS", "GZ", "LB")
FRONT_STAGES = ("FQ0", "FK0", "FQ1", "FK1", "FV0", "FV1", "XS", "SQ0", "SK0", "SQ1", "SK1")
AT_FIRST = {
    "FQ0": -13, "FK0": -11, "FQ1": -6, "FK1": -5, "FV0": 19, "FV1": 24, "SQ0": -8, "SK0": -7, "SQ1": -3, "SK1": -3,
    "XS": -19,
}
AT_LAST = {
    "VT": 4, "OP0": 4, "OP1": 8, "HT": 12, "RQ0": 12, "RQ1": 12, "RK0": 12, "RK1": 12, "RV0": 15, "RV1": 16,
    "KT0": 16, "KT1": 16, "KV0": 23, "KV1": 24, "A00": 28, "A01": 28, "Y00": 28, "A02": 28, "Y01": 28, "A03": 28,
    "Y02": 29, "A10": 34, "Y03": 34, "A11": 34, "Y10": 34, "A12": 34, "Y11": 34, "A13": 34, "Y12": 34, "Y13": 34,
    "GM": 35, "GV": 37, "WO0": 40, "WO1": 40, "HU": 47, "U1": 52, "H0": 53, "H1": 54, "H2": 54, "Q0": 54, "H3": 54,
    "Q1": 54, "H4": 54, "Q2": 54, "H5": 54, "Q3": 54, "H6": 54, "Q4": 54, "H7": 54, "Q5": 54, "Q6": 55, "Q7": 56,
    "V0": 57, "V1": 58, "LA": 10, "SS": 26, "GZ": 38, "LB": 45,
}
AT_DELAYED = {
    "HU": 1, "U1": 1, "H0": 4, "H1": 4, "H2": 8, "Q0": 8, "H3": 8, "Q1": 8, "H4": 8, "Q2": 9, "H5": 9, "Q3": 9,
    "H6": 34, "Q4": 34, "H7": 34, "Q5": 35, "Q6": 37, "Q7": 37, "V0": 39, "V1": 40,
}
PAIRS = ("VT", "HT", "HU")
CLS_START = {"C0": 29, "C1": 34, "C2": 39, "C3": 41, "C4": 43}
CLS_END = {"CW": 52, "CT": 53, "CU": 54, "CH": 55, "CQ": 56, "CV": 63}
NR_LAG = 4
MT_EARLY = 6
REP, REP_FIRST = [34, 7], [-44, -40]
V_COPY, V_COPY_FIRST = [40, 1], [-25, -3]
REST_LOAD, CLASS_NORM = 5, 25
W_SPLIT = [-40, -40, -39, 30, 33, 34, 37, 38, 39, 40]
X_LOAD, X_LOAD_FIRST = 61, -42


def stages(it):
    out = []
    for t in range(STEPS):
        step = STEPS * it + t
        if it == 0:
            out += [(t, name, 0) for name, at in CLS_START.items() if at == t]
        if step >= GS + NR_LAG and (step - NR_LAG) % GS == 0 and (step - NR_LAG) // GS - 1 < B * NG:
            out.append((t, "NR", (step - NR_LAG) // GS - 1))
        for name in AT:
            front = name in FRONT_STAGES
            if front and step == AT_FIRST[name]:
                out.append((t, name, 1))
            b = it + 1 if front else it - 1
            if it == B and t == AT_DELAYED.get(name):
                out += [(t, f"{name}{ft}", B - 2) for ft in range(KC)] if name in PAIRS else [(t, name, B - 2)]
            if b == B - 2 and name in AT_DELAYED:
                continue
            at = (AT_LAST if b == B - 1 and not front else AT)[name]
            if not 0 <= b < B or (front and b == 1):
                continue
            if at == t:
                out += [(t, f"{name}{ft}", b) for ft in range(KC)] if name in PAIRS else [(t, name, b)]
        if it == B:
            out += [(t, name, 0) for name, at in CLS_END.items() if at == t]
        if (step + MT_EARLY) % GS == 0 and 0 <= (step + MT_EARLY) // GS < B * NG:
            out.append((t, "MT", (step + MT_EARLY) // GS))
    return out


def product_of(name, b):
    return (name[:2] if name[0] == "Y" else "U2" if name[0] == "Q" else name, b)


def banks():
    order = [product_of(name, b) for it in range(-1, B + 1) for _, name, b in stages(it) if name not in BESIDE]
    final = {key: i for i, key in enumerate(order)}
    use, held, given_up, uses = {}, set(), [0] * 3, [0] * 3
    for i, key in enumerate(order):
        if key not in use:
            bank = min((n for n in range(3) if n not in held), key=lambda n: given_up[n])
            use[key] = (bank, uses[bank])
            uses[bank] += 1
            held.add(bank)
        if i == final[key]:
            bank = use[key][0]
            held.remove(bank)
            given_up[bank] = i + 1
    return use


Tail = namedtuple("Tail", "h hn hT hid qT rqT rkT rv ktok state")


def repeat(ap, axis, n):
    shape = list(ap.shape)
    shape[axis] = n
    return ap.broadcast_to(shape)


def offsets(pack):
    at, out = 0, {}
    for name, n in pack:
        out[name] = slice(at, at + n)
        at += n
    return out, at


def vit_tower(nc, xt, front_weights, front, rest, weights, cls, out):
    foff, fcols = offsets(FRONT)
    roff, rcols = offsets(REST)
    woff, wcols = offsets(WEIGHTS)
    front_cols = woff["wv"].stop

    use = banks()

    with ExitStack() as ctx:
        def sb(name, shape, dt=F32):
            return ctx.enter_context(nc.sbuf_tensor(name, shape, dt))

        def sem(name):
            return ctx.enter_context(nc.semaphore(name))

        fpack = sb("fpack", [P, fcols])
        rpack = sb("rpack", [P, rcols])

        def w(name, split=None):
            ap = fpack[:, foff[name]] if name in foff else rpack[:, roff[name]]
            return ap.rearrange("p (a b) -> p a b", a=split) if split else ap

        weight_parts = [sb("weights_high", [P, wcols], F32R), sb("weights_low", [P, wcols], F32R)]
        v1 = [part[:, woff["v1"]] for part in weight_parts]
        wq, wk, wv, wout, rwq, rwk, rwv, rwo, u1 = (
            [part[:, woff[n]].rearrange("p (a b) -> p a b", a=KC) for part in weight_parts]
            for n in ("wq", "wk", "wv", "wout", "rwq", "rwk", "rwv", "rwo", "u1"))
        gq, gk = w("gq", KC), w("gk", KC)
        u2 = w("u2", FT)
        ident = w("ident")
        identb = sb("identb", [P, P], BF16)
        x_parts = [sb("x_high", [P, KC, S], F32R), sb("x_low", [P, KC, S], F32R)]
        qkf = sb("qkf", [P, KC, S])
        split = sb("split", [P, 2, 3, KC, S], BF16)
        qr = sb("qr", [KM, NH, S], BF16)
        kr = sb("kr", [KM, NH, S], BF16)
        vstage = sb("vstage", [P, QT, D])
        vaug = sb("vaug", [P, QT, NH, 32])
        probs = sb("probs", [P, 2, HG, S])
        negmax = sb("negmax", [P, 2, GS])
        mparts = sb("mparts", [P, 2, GS], BF16)
        mrows = sb("mrows", [2 * GS, P], BF16)
        oT = sb("oT", [P, S])
        rsum = sb("rsum", [P, QT, HG])
        vals = sb("vals", [P, QT, D])
        h = sb("h", [P, QT, D])
        hn = sb("hn", [P, QT, D])
        hT = [sb("hT_high", [P, KC, S], F32R), sb("hT_low", [P, KC, S], F32R)]
        bst = sb("bst", [P, QT, 6])
        mv = sb("mv", [P, QT, 2])
        rstd = sb("rstd", [P, QT])
        mhalf = sb("mhalf", [P, QT])
        hbias = sb("hbias", [P, 2, KC])
        qblk = sb("qblk", [P, KC, RQ, S])
        first_state = sb("first_state", [P, KC, P])
        xT = hn[:, :, :].rearrange("p a b -> p (a b)").rearrange("p (a b) -> p a b", a=KC)
        zc = sb("zc", [P, 2, KC, B], F32R)
        yc = sb("yc", [P, KC])
        gst = sb("gst", [P, KC, 2, 6])
        gmv = sb("gmv", [P, KC, 2])
        gmu = sb("gmu", [P, KC])
        gd = sb("gd", [P, KC])
        gvar = sb("gvar", [P, KC])
        grs = sb("grs", [P, KC])
        gscale = sb("gscale", [P, KC])
        gshift = sb("gshift", [P, KC])
        p_parts = sb("p_parts", [P, S], F32R)
        hid = sb("hid", [P, FT, S])
        staged = [hid[:, :, :].rearrange("p a b -> p (a b)")[:, 0:n] for n in (front_cols, wcols - front_cols)]

        def whole(name):
            at = woff[name]
            later = at.start >= front_cols
            return staged[later][:, at.start - front_cols * later:at.stop - front_cols * later]

        amask = qkf[:, :, :].rearrange("p a (j n) -> p a j n", j=RQ)
        y = sb("y", [P, KC, S + 1])
        qT = y[:, 0, 0:S]
        kvm = y[:, :, 0:3 * P].rearrange("p f (c n) -> p f c n", c=3)
        z = [sb("z_high", [P, KC, S + 1], F32R), sb("z_low", [P, KC, S + 1], F32R)]
        vT = [part[:, :, 0:S] for part in z]

        def tail_buffers(h, hn, hT, hid, qT):
            later = hn[:, 0:3, :].rearrange("p c (a b) -> p c a b", a=KC)
            return Tail(h, hn, hT, hid, qT, hid[:, 0:2, :], hid[:, 2:4, :],
                        hid[:, 4:6, :].rearrange("p a (c n) -> p (a c) n", n=D),
                        hid[:, 6:8, :].rearrange("p a (c n) -> p (a c) n", n=D),
                        [first_state[:, :, :]] + [later[:, c] for c in range(3)])

        spare = vaug[:, :, :, :].rearrange("p q n c -> p (q n c)").rearrange("p (i q n) -> p i q n", i=2, q=QT)
        tails = [tail_buffers(h, hn, hT, hid, qT)] * (B - 2)
        tails.append(tail_buffers(h, hn, hT, hid, oT[:, :]))
        tails.append(tail_buffers(spare[:, 0], spare[:, 1], x_parts,
                                  probs[:, :, :, :].rearrange("p a j s -> p (a j) s"), qT))
        crow, crow_end = hn[0:B], vstage[0:B]
        clsrow, clsrow_end = crow[:, 3, :], crow_end[:, 1, :]
        cst = sb("cst", [B, 6])
        cmv = sb("cmv", [B, 4])
        cT = sb("cT", [P, 2, KC])
        cTp = sb("cTp", [P, 2, KC, B], F32R)
        one = sb("one", [P, 1])
        cP = sb("cP", [P, B], F32R)
        chid = qkf[:, 0, 0:FT * B].rearrange("p (f b) -> p f b", b=B)
        cQ = qkf[:, 1, 0:B]

        st_ps = ctx.enter_context(nc.psum_tensor("st_ps", [P, 2, S], F32))
        mx_ps = ctx.enter_context(nc.psum_tensor("mx_ps", [P, 2, S], F32))
        pv_ps = ctx.enter_context(nc.psum_tensor("pv_ps", [P, S], F32))
        ps = [ctx.enter_context(nc.psum_tensor(f"ps{i}", [P, S], F32)) for i in range(3)]

        front_in, small_in, wv_in, rest_in, cls_in = sem("front_in"), sem("small_in"), sem("wv_in"), sem("rest_in"), sem("cls_in")
        x_in, x_high, x_low = sem("x_in"), sem("x_high"), sem("x_low")
        full = [sem(f"full{i}") for i in range(3)]
        drained = [sem(f"drained{i}") for i in range(3)]
        max_full, max_done = sem("max_full"), sem("max_done")
        st_full, exp_done = sem("st_full"), sem("exp_done")
        pv_done, o_ready = sem("pv_done"), sem("o_ready")
        m_split, m_rows = sem("m_split"), sem("m_rows")
        qk_parts = sem("qk_parts")
        first_part, qk_rest, second_part = sem("first_part"), sem("qk_rest"), sem("second_part")
        rep = [sem("rep0"), sem("rep1")]
        v_half = sem("v_half")
        ln_stats, ln_rstd, ln_done = sem("ln_stats"), sem("ln_rstd"), sem("ln_done")
        hb_done = sem("hb_done")
        qblk_in = sem("qblk_in")
        states = sem("states")
        z_whole = sem("z_whole")
        y_chunk = sem("y_chunk")
        w_high, w_low = sem("w_high"), sem("w_low")
        t_high, z_high = sem("t_high"), sem("z_high")
        g_mean, g_dev, g_rstd, z_done, zc_done = sem("g_mean"), sem("g_dev"), sem("g_rstd"), sem("z_done"), sem("zc_done")
        out_done = sem("out_done")
        consts, vconst = sem("consts"), sem("vconst")
        ones_done, zeros_done = sem("ones_done"), sem("zeros_done")
        c_hn, c_rstd, c_gelu, c_out, c_var = sem("c_hn"), sem("c_rstd"), sem("c_gelu"), sem("c_out"), sem("c_var")
        v_chain, halves_set = sem("v_chain"), sem("halves_set")

        def bank(key):
            return ps[use[key][0]]

        def wait_full(eng, key):
            i, n = use[key]
            eng.wait_ge(full[i], n + 1)

        def wait_drained(eng, key):
            i, n = use[key]
            eng.wait_ge(drained[i], n + 1)

        def wait_free(pe, key):
            i, n = use[key]
            if n:
                pe.wait_ge(drained[i], n)

        def inc_full(ins, key):
            ins.then_inc(full[use[key][0]], 1)

        def inc_drained(ins, key):
            ins.then_inc(drained[use[key][0]], 1)

        vcount = [0]

        def vlink(ins):
            vcount[0] += 1
            ins.then_inc(v_chain, 1)
            nc.vector.wait_ge(v_chain, vcount[0])

        highs = {}
        for it in range(-1, B + 1):
            for _, name, b in stages(it):
                if name[:2] in PAIRS:
                    highs[name, b] = len(highs) + 1

        walk = [(it, t, STEPS * it + t, [(n, b) for u, n, b in stages(it) if u == t])
                for it in range(-1, B + 1) for t in range(STEPS)]
        block = ctx.enter_context(nc.Block())

        @block.sync
        def _(sp):
            first = woff["wk"].stop
            sp.dma_start(staged[0][:, 0:first], front_weights[:, 0:first]).then_inc(front_in, 16)
            sp.dma_start(xT, xt[0]).then_inc(x_in, 16)
            sp.dma_start(fpack[:, :], front).then_inc(small_in, 16)
            sp.dma_start(staged[0][:, first:], front_weights[:, first:]).then_inc(wv_in, 16)
            for it, t, step, todo in walk:
                for half in range(2):
                    b = it + 1 - half
                    if step == REP_FIRST[half]:
                        b = 0
                    elif t != REP[half] or not 1 <= b < B:
                        continue
                    if b:
                        sp.wait_ge(st_full, STEPS * b - (STEPS // 2 if half == 0 else 0))
                    for i, (dst, part) in enumerate(((qr, Q_PART), (kr, K_PART))):
                        sp.wait_ge(qk_parts, 4 * b + 2 * half + i + 1)
                        for g in range(PARTS):
                            sp.dma_start(dst[HD * g:HD * (g + 1), HH * half:HH * (half + 1), :],
                                         split[:, i, part[g], half, :]).then_inc(rep[half], 16)
                if step == REST_LOAD:
                    sp.dma_start(rpack[:, :], rest).then_inc(rest_in, 16)
                    sp.wait_ge(w_low, len(FRONT_WEIGHTS))
                    sp.dma_start(staged[1], weights).then_inc(rest_in, 16)
                if step == CLASS_NORM - 12:
                    sp.wait_ge(x_low, KC)
                    sp.dma_start(clsrow, cls).then_inc(cls_in, 16)
                if step == STEPS * B:
                    sp.wait_ge(v_half, 2 * B)
                    sp.dma_start(clsrow_end, cls).then_inc(cls_in, 16)
                for name, b in todo:
                    if name == "MT":
                        wait_drained(sp, (name, b))
                        if b >= NG:
                            sp.wait_ge(st_full, GS * (b - NG + 1))
                        g = b % NG
                        for i in range(2):
                            sp.dma_start(qr[KR + i:KR + i + 1, HG * g:HG * (g + 1), :],
                                         mrows[GS * i:GS * (i + 1), :]).then_inc(m_rows, 16)
                    if name == "RQ1":
                        wait_drained(sp, ("RQ0", b))
                        wait_drained(sp, ("RQ1", b))
                        sp.wait_ge(zeros_done, 1)
                        if b:
                            wait_full(sp, ("A13", b - 1))
                        for j in range(RQ):
                            sp.dma_start(qblk[RD * j:RD * (j + 1), :, j, :],
                                         tails[b].rqT[RD * j:RD * (j + 1), :, :]).then_inc(qblk_in, 16)
                    if name in ("V0", "V1"):
                        i = int(name[1])
                        wait_drained(sp, (name, b))
                        sp.dma_start(out[b, 1 + i * 2 * P:1 + (i + 1) * 2 * P, :].rearrange("(a p) n -> p a n", p=P),
                                     tails[b].hn[:, 2 * i:2 * i + 2, :]).then_inc(out_done, 16)
                    if name == "CV":
                        sp.wait_ge(c_out, 1)
                        sp.dma_start(out[:, 0, :], crow_end[:, 2, :]).then_inc(out_done, 16)
                if step == X_LOAD_FIRST or it >= 0 and t == X_LOAD and it + 2 < B:
                    b = 1 if it < 0 else it + 2
                    if b == 1:
                        wait_full(sp, ("FV1", 0))
                    elif b == 2:
                        wait_full(sp, ("C4", 0))
                    else:
                        sp.wait_ge(out_done, 32 * (b - 2))
                    sp.dma_start(xT, xt[b]).then_inc(x_in, 16)
            sp.wait_ge(out_done, 16 * (2 * B + 1))

        @block.tensor
        def _(pe):
            def mm(o, a, b, start, stop, check=False):
                return nc.tensor.matmul(o, a, b, start=start, stop=stop, skip_group_check=check)

            def product(o, a, b, left, right, low_ready=None, order=((0, 0), (0, 1), (1, 0))):
                pairs = [(a[i], b[j]) for i, j in order] if isinstance(a, list) else [(a, b)]
                for n, (x, y) in enumerate(pairs):
                    if n == len(pairs) - 1 and low_ready:
                        low_ready()
                    for k in range(KC):
                        last = mm(o, x[:, k, left], y[:, k, right], n + k == 0, n + k == len(pairs) + KC - 2)
                return last

            def tokens_out(key, lhs, weights, i, low_ready=None):
                for a in range(2):
                    last = product(bank(key)[:, a * D:(a + 1) * D], lhs, weights,
                                   slice((2 * i + a) * P, (2 * i + a + 1) * P), slice(0, D), low_ready)
                inc_full(last, key)

            def features_out(key, weights, rhs, ft, low_ready=None):
                inc_full(product(bank(key)[:, :], weights, rhs, slice(ft * P, (ft + 1) * P), slice(0, S), low_ready,
                                 ((0, 0), (1, 0), (0, 1))), key)

            def transposes(keys, src, ready=None, before=0):
                for q in range(QT):
                    if ready:
                        pe.wait_ge(ready, before + q + 1)
                    for ft in range(KC):
                        if q == 0:
                            wait_free(pe, keys[ft])
                        last = nc.tensor.transpose(bank(keys[ft])[:, q * P:(q + 1) * P],
                                                   src[:, q, ft * P:(ft + 1) * P], ident)
                        if q == QT - 1:
                            inc_full(last, keys[ft])

            def both_drained(pair, b):
                return lambda: [wait_drained(pe, (pair + str(ft), b)) for ft in range(KC)]

            fwq, fwk, fwv = (whole(n).rearrange("p (a b) -> p a b", a=KC) for n in ("rwq", "rwk", "rwv"))

            def stage(name, b):
                key = product_of(name, b)
                if name in ("VT1", "HT1", "HU1") or name in BESIDE:
                    return
                if name in ("VT0", "HT0", "HU0"):
                    keys = [(name[:2] + str(ft), b) for ft in range(KC)]
                    if name == "VT0":
                        wait_drained(pe, ("NR", NG * b + NG - 1))
                        transposes(keys, vals)
                    else:
                        transposes(keys, tails[b].hn, ln_done, QT * (2 * b + (name == "HU0")))
                    return
                if name[0] not in "YQ" or name[-1] == "0":
                    wait_free(pe, key)
                o = bank(key)
                if name == "MT":
                    pe.wait_ge(m_split, b + 1)
                    pe.wait_ge(consts, 3)
                    inc_full(nc.tensor.transpose(o[:, 0:P // 2].bitcast(BF16)[0:2 * GS, :],
                                                 mparts[:, :, :].rearrange("p a b -> p (a b)"), identb[:, :]), key)
                elif name == "NR":
                    pe.wait_ge(o_ready, b + 1)
                    for q in range(QT):
                        last = nc.tensor.transpose(o[:, q * P:(q + 1) * P], oT[:, q * P:(q + 1) * P], ident)
                    inc_full(last, key)
                elif name in ("FQ0", "FQ1", "FK0", "FK1"):
                    if b == 0:
                        if name == "FQ0":
                            pe.wait_ge(front_in, 16)
                            pe.wait_ge(x_in, 16)
                        weights = whole("wq" if name[1] == "Q" else "wk").rearrange("p (a b) -> p a b", a=KC)
                        features_out(key, weights, xT, int(name[2]))
                    else:
                        pe.wait_ge(x_low, KC * b)
                        features_out(key, wq if name[1] == "Q" else wk, x_parts, int(name[2]))
                elif name in ("FV0", "FV1"):
                    if b == 0:
                        pe.wait_ge(wv_in, 16)
                        tokens_out(key, xT, whole("wv").rearrange("p (a b) -> p a b", a=KC), int(name[2]))
                    else:
                        pe.wait_ge(x_low, KC * b)
                        tokens_out(key, x_parts, wv, int(name[2]))
                elif name in ("OP0", "OP1"):
                    if name == "OP0":
                        pe.wait_ge(rest_in, 32)
                        pe.wait_ge(w_low, len(WEIGHTS))
                        pe.wait_ge(t_high, highs["VT1", b])
                    tokens_out(key, vT, wout, int(name[2]), both_drained("VT", b))
                elif name in ("RQ0", "RQ1", "RK0", "RK1"):
                    if name == "RQ0":
                        pe.wait_ge(t_high, highs["HT1", b])
                    features_out(key, rwq if name[1] == "Q" else rwk, tails[b].hT, int(name[2]), both_drained("HT", b))
                elif name in ("RV0", "RV1"):
                    tokens_out(key, tails[b].hT, rwv, int(name[2]), both_drained("HT", b))
                elif name in ("KT0", "KT1"):
                    if name == "KT0":
                        wait_drained(pe, ("RK0", b))
                        wait_drained(pe, ("RK1", b))
                    for a, c in enumerate(range(2) if name == "KT0" else range(2, 3)):
                        for ft in range(KC):
                            last = nc.tensor.transpose(o[:, a * D + ft * P:a * D + (ft + 1) * P],
                                                       tails[b].rkT[:, ft, c * P:(c + 1) * P], ident)
                    inc_full(last, key)
                elif name in ("KV0", "KV1"):
                    ft = int(name[2])
                    if ft == 0:
                        for n in ("RV0", "RV1", "KT0", "KT1"):
                            wait_drained(pe, (n, b))
                    for c in range(3):
                        last = mm(o[:, c * P:(c + 1) * P], tails[b].ktok[:, c, ft * P:(ft + 1) * P],
                                  tails[b].rv[:, c, ft * P:(ft + 1) * P], True, True)
                    inc_full(last, key)
                elif name[0] == "A":
                    ft, c = int(name[1]), int(name[2])
                    if name == "A00":
                        pe.wait_ge(qblk_in, 64 * (b + 1))
                    inc_full(mm(o[:, :], tails[b].rkT[:, ft, c * P:(c + 1) * P], qblk[:, ft, :, c * P:(c + 1) * P], True, True), key)
                elif name[0] == "Y":
                    ft, c = int(name[1]), int(name[2])
                    if name == "Y00":
                        pe.wait_ge(states, KC * (b + 1))
                    at = slice(c * P, (c + 1) * P)
                    mm(o[:, at], tails[b].state[c][:, ft, :], tails[b].rqT[:, ft, at], True, False, True)
                    wait_drained(pe, (f"A{ft}{c}", b))
                    for j in range(RQ):
                        last = mm(o[RD * j:RD * (j + 1), at], tails[b].rv[:, c, ft * P + RD * j:ft * P + RD * (j + 1)],
                                  amask[:, c % 2, j, :], False, True, True)
                    if c == 3:
                        inc_full(last, key)
                    else:
                        last.then_inc(y_chunk, 1)
                elif name == "GM":
                    pe.wait_ge(g_mean, b + 1)
                    inc_full(mm(o[:, 0:KC], w("headmean"), gmv[:, :, 0], True, True), key)
                elif name == "GV":
                    pe.wait_ge(g_dev, b + 1)
                    inc_full(mm(o[:, 0:KC], w("headmean"), gd[:, :], True, True), key)
                elif name in ("WO0", "WO1"):
                    if name == "WO0":
                        pe.wait_ge(z_high, KC * (b + 1))
                    tokens_out(key, z, rwo, int(name[2]), lambda: pe.wait_ge(z_done, KC * (b + 1)))
                elif name == "U1":
                    pe.wait_ge(t_high, highs["HU1", b])
                    features_out(key, u1, tails[b].hT, 0, both_drained("HU", b))
                elif name[0] == "H" and name[1].isdigit():
                    f = int(name[1])
                    if f == 0:
                        wait_drained(pe, ("U1", b))
                    at = slice(f * P, (f + 1) * P)
                    mm(o[:, :], v1[0][:, at], p_parts[:, :], True, False)
                    inc_full(mm(o[:, :], v1[1][:, at], p_parts[:, :], False, True), key)
                elif name[0] == "Q":
                    f = int(name[1])
                    wait_drained(pe, (f"H{f}", b))
                    i = f % 2
                    last = mm(o[RANK * i:RANK * (i + 1), :], u2[:, f, :], tails[b].hid[:, f, :], f < 2, f >= FT - 2, True)
                    if f == FT - 1:
                        inc_full(last, key)
                elif name in ("V0", "V1"):
                    i = int(name[1])
                    if i == 0:
                        wait_drained(pe, ("U2", b))
                    for a in range(2):
                        last = mm(o[:, a * D:(a + 1) * D], tails[b].qT[:, (2 * i + a) * P:(2 * i + a + 1) * P], w("v2"), True, True)
                    inc_full(last, key)
                elif name == "C0":
                    pe.wait_ge(c_hn, 1)
                    for k in range(KC):
                        last = mm(o[:, k:k + 1], crow[0:1, 0, k * P:(k + 1) * P], one[0:1, :], True, True)
                    inc_full(last, key)
                elif name == "C1":
                    wait_drained(pe, ("C0", 0))
                    pe.wait_ge(rest_in, 32)
                    for ft in range(KC):
                        for k in range(KC):
                            last = mm(o[:, ft:ft + 1], fwq[:, k, ft * P:(ft + 1) * P], cT[:, 0, k:k + 1], k == 0, k == KC - 1)
                    inc_full(last, key)
                elif name == "C2":
                    for i, weights in enumerate((fwk, fwv)):
                        for k in range(KC):
                            last = mm(o[0:1, i * D:(i + 1) * D], cT[:, 0, k:k + 1], weights[:, k, :], k == 0, k == KC - 1)
                    inc_full(last, key)
                elif name == "C3":
                    wait_drained(pe, ("C2", 0))
                    for ft in range(KC):
                        at = slice(ft * P, (ft + 1) * P)
                        last = mm(o[:, at], crow[0:1, 1, at], crow[0:1, 2, at], True, True)
                    inc_full(last, key)
                elif name == "C4":
                    wait_drained(pe, ("C1", 0))
                    wait_drained(pe, ("C3", 0))
                    for ft in range(KC):
                        last = mm(o[:, ft:ft + 1], tails[b].state[0][:, ft, :], cT[:, 1, ft:ft + 1], True, True)
                    inc_full(last, key)
                elif name == "CW":
                    pe.wait_ge(zc_done, 2 * B)
                    inc_full(product(o[0:B, 0:D], [zc[:, 0], zc[:, 1]], rwo, slice(0, B), slice(0, D)), key)
                elif name == "CT":
                    pe.wait_ge(c_hn, 2)
                    for k in range(KC):
                        last = mm(o[:, k * B:(k + 1) * B], crow_end[0:B, 0, k * P:(k + 1) * P], w("ident")[0:B, 0:B], True, True)
                    inc_full(last, key)
                elif name == "CU":
                    wait_drained(pe, ("CT", 0))
                    inc_full(product(o[:, 0:B], u1, [cTp[:, 0], cTp[:, 1]], slice(0, P), slice(0, B)), key)
                elif name == "CH":
                    wait_drained(pe, ("CU", 0))
                    for f in range(FT):
                        at = slice(f * P, (f + 1) * P)
                        mm(o[:, f * B:(f + 1) * B], v1[0][:, at], cP[:, :], True, False)
                        last = mm(o[:, f * B:(f + 1) * B], v1[1][:, at], cP[:, :], False, True)
                    inc_full(last, key)
                elif name == "CQ":
                    pe.wait_ge(c_gelu, 1)
                    for f in range(FT):
                        i = f % 2
                        last = mm(o[RANK * i:RANK * (i + 1), 0:B], u2[:, f, :], chid[:, f, :], f < 2, f >= FT - 2, True)
                    inc_full(last, key)
                elif name == "CV":
                    wait_drained(pe, ("CQ", 0))
                    inc_full(mm(o[0:B, 0:D], cQ, w("v2"), True, True), key)
                else:
                    raise ValueError(name)

            for it, t, step, todo in walk:
                m = step + AHEAD
                if 0 <= m < B * STEPS:
                    head, q = m % STEPS // QT, m % QT
                    if m % STEPS in (0, STEPS // 2):
                        pe.wait_ge(rep[m % STEPS // (STEPS // 2)], 16 * 2 * PARTS * (m // STEPS + 1))
                    if m >= 2:
                        pe.wait_ge(max_done, m - 1)
                    mm(mx_ps[:, m % 2, :], qr[0:KR, head, q * P:(q + 1) * P], kr[0:KR, head, :], True, True)\
                        .then_inc(max_full, 1)
                if 0 <= step < B * STEPS:
                    n, kt, j = step // GS, step % GS // HG, step % HG
                    head = HG * (n % NG) + j
                    if step % GS == 0:
                        pe.wait_ge(m_rows, 32 * (n + 1))
                        pe.wait_ge(ones_done, 1)
                    if step >= 2:
                        pe.wait_ge(exp_done, step - 1)
                    mm(st_ps[:, step % 2, :], kr[:, head, kt * P:(kt + 1) * P], qr[:, head, :], True, True)\
                        .then_inc(st_full, 1)
                last_exp = step - PV_LAG
                if 0 <= last_exp < B * STEPS and last_exp % HG == HG - 1:
                    n, kt = last_exp // GS, last_exp % GS // HG
                    pe.wait_ge(exp_done, last_exp + 1)
                    if kt == 0 and n % (NG // 2) == 0:
                        pe.wait_ge(v_half, n // (NG // 2) + 1)
                    if kt == 0 and n:
                        pe.wait_ge(o_ready, n)
                    for j in range(HG):
                        last = mm(pv_ps[32 * j:32 * (j + 1), :], vaug[:, kt, HG * (n % NG) + j, :], probs[:, kt % 2, j, :],
                                  kt == 0, kt == QT - 1)
                    last.then_inc(pv_done, 1)
                for name, b in todo:
                    stage(name, b)

        @block.scalar
        def _(act):
            def stage(name, b):
                key = (name, b)
                if name in ("FQ0", "FQ1", "FK0", "FK1"):
                    wait_full(act, key)
                    i, half = int(name[1] == "K"), int(name[2])
                    if 4 * b + 2 * half:
                        act.wait_ge(qk_parts, 4 * b + 2 * half - 1 + i)
                    if name == "FQ0" and b == 0:
                        act.wait_ge(consts, 3)
                    if b:
                        act.wait_ge(rep[half], 16 * 2 * PARTS * b)
                        nc.scalar.activation(split[:, i, 0, half, :], bank(key)[:, :], ACT.Identity,
                                             bias=hbias[:, i, half:half + 1], scale=0.5).then_inc(first_part, 1)
                    inc_drained(nc.scalar.activation(qkf[:, i, :], bank(key)[:, :], ACT.Identity,
                                                     bias=hbias[:, i, half:half + 1], scale=0.5), key)
                elif name in ("SQ0", "SK0", "SQ1", "SK1") and b:
                    i, half = int(name[1] == "K"), int(name[2])
                    act.wait_ge(qk_rest, 4 * (b - 1) + 2 * half + i + 1)
                    nc.scalar.copy(split[:, i, 1, half, :], qkf[:, i, :]).then_inc(second_part, 1)
                elif name in ("FV0", "FV1"):
                    wait_full(act, key)
                    if b:
                        act.wait_ge(v_half, 2 * b)
                    i = int(name[2])
                    inc_drained(nc.scalar.copy(vstage[:, 2 * i:2 * i + 2, :].rearrange("p a b -> p (a b)"),
                                               bank(key)[:, :]), key)
                elif name[:2] in PAIRS:
                    wait_full(act, key)
                    if name[:2] == "HU":
                        wait_full(act, ("RV1", b))
                    elif name[:2] == "HT" and b == B - 1:
                        wait_full(act, ("FV1", b))
                    elif b:
                        wait_full(act, ("WO1" if name[:2] == "VT" else "U1", b - 1))
                    if name[:2] == "VT" and b:
                        act.wait_ge(zc_done, 2 * b)
                    dst = (vT if name[:2] == "VT" else tails[b].hT)[0]
                    nc.scalar.copy(dst[:, int(name[2]), :], bank(key)[:, :]).then_inc(t_high, 1)
                elif name == "XS" and b:
                    act.wait_ge(x_in, 16 * (b + 1))
                    if b > 1:
                        wait_full(act, ("FV1", b - 1))
                    for k in range(KC):
                        nc.scalar.copy(x_parts[0][:, k, :], xT[:, k, :]).then_inc(x_high, 1)
                elif name == "GZ":
                    for ft in range(KC):
                        act.wait_ge(z_whole, KC * b + ft + 1)
                        nc.scalar.copy(z[0][:, ft, :], y[:, ft, :]).then_inc(z_high, 1)
                elif name in ("RV0", "RV1"):
                    wait_full(act, key)
                    if b:
                        wait_full(act, ("Y1", b - 1))
                    i = int(name[2])
                    inc_drained(nc.scalar.copy(tails[b].rv[:, 2 * i:2 * i + 2, :].rearrange("p a b -> p (a b)"), bank(key)[:, :]), key)
                elif name in ("KT0", "KT1"):
                    wait_full(act, key)
                    if b:
                        wait_full(act, ("KV1", b - 1))
                    c, n = (0, 2) if name == "KT0" else (2, 1)
                    inc_drained(nc.scalar.copy(tails[b].ktok[:, c:c + n, :].rearrange("p a b -> p (a b)"), bank(key)[:, 0:n * D]), key)
                elif name in ("Y03", "Y13"):
                    ft = int(name[1])
                    wait_full(act, (name[:2], b))
                    if b:
                        act.wait_ge(z_done, KC * b)
                        act.wait_ge(g_mean, b)
                    inc_drained(nc.scalar.copy(y[:, ft, 0:S], bank((name[:2], b))[:, :]), (name[:2], b))
                elif name[0] == "H" and name[1].isdigit():
                    f = int(name[1])
                    wait_full(act, key)
                    inc_drained(nc.scalar.activation(tails[b].hid[:, f, :], bank(key)[:, :], ACT.Gelu_apprx_tanh,
                                                     bias=w("b1")[:, f:f + 1]), key)
                elif name == "Q7":
                    key = ("U2", b)
                    wait_full(act, key)
                    if b == B - 2:
                        wait_full(act, ("NR", B * NG - 1))
                    inc_drained(nc.scalar.copy(tails[b].qT, bank(key)[:, :]), key)
                elif name == "CH":
                    wait_drained(act, key)
                    nc.scalar.activation(chid, chid, ACT.Gelu_apprx_tanh).then_inc(c_gelu, 1)

            for it, t, step, todo in walk:
                for i, at in enumerate(W_SPLIT):
                    if step == at:
                        if i == 0:
                            act.wait_ge(front_in, 16)
                            act.wait_ge(wv_in, 16)
                        elif i == len(FRONT_WEIGHTS):
                            act.wait_ge(rest_in, 32)
                        name = WEIGHTS[i][0]
                        nc.scalar.copy(weight_parts[0][:, woff[name]], whole(name)).then_inc(w_high, 1)
                if 0 <= step < B * STEPS:
                    n, kt, j = step // GS, step % GS // HG, step % HG
                    act.wait_ge(st_full, step + 1)
                    if step // HG >= 2 and j == 0:
                        act.wait_ge(pv_done, step // HG - 1)
                    nc.scalar.activation(probs[:, kt % 2, j, :], st_ps[:, step % 2, :], ACT.Exp).then_inc(exp_done, 1)
                n = (step - PV_LAG) // GS
                if 0 <= n < B * NG and (step - PV_LAG) % GS == GS - 1:
                    act.wait_ge(pv_done, QT * (n + 1))
                    if n:
                        wait_full(act, ("NR", n - 1))
                    nc.scalar.copy(oT[:, :], pv_ps[:, :]).then_inc(o_ready, 1)
                for name, b in todo:
                    stage(name, b)

        @block.vector
        def _(dve):
            dve.wait_ge(small_in, 16)
            nc.vector.tensor_copy(identb[:, :], ident).then_inc(consts, 1)
            for i, name in enumerate(("qbias", "kbias")):
                nc.vector.tensor_scalar(hbias[:, i, :], w(name), 0.5, None, ALU.mult).then_inc(consts, 1)
            def row_stats(src, n):
                vlink(nc.vector.bn_stats(cst[0:n, :], src))
                vlink(nc.vector.bn_aggr(cmv[0:n, 0:2], cst[0:n, :]))
                nc.vector.tensor_scalar(cmv[0:n, 2:3], cmv[0:n, 1:2], EPS, None, ALU.add).then_inc(c_var, 1)

            def row_norm(src, dst, n, count):
                dve.wait_ge(c_rstd, count)
                nc.vector.tensor_scalar(dst, src, cmv[0:n, 0:1], cmv[0:n, 3:4],
                                        ALU.subtract, ALU.mult).then_inc(c_hn, 1)

            def class_norm():
                dve.wait_ge(cls_in, 16)
                row_stats(clsrow[0:1], 1)
                row_norm(clsrow[0:1], crow[0:1, 0, :], 1, 1)

            def layer_norm_stats(key, i, b):
                wait_drained(dve, key)
                for q in (2 * i, 2 * i + 1):
                    nc.vector.bn_stats(bst[:, q, :], tails[b].h[:, q, :]).then_inc(v_chain, 1)
                vcount[0] += 2
                dve.wait_ge(v_chain, vcount[0])
                for q in (2 * i, 2 * i + 1):
                    nc.vector.bn_aggr(mv[:, q, :], bst[:, q, :]).then_inc(v_chain, 1)
                vcount[0] += 2
                dve.wait_ge(v_chain, vcount[0])
                nc.vector.tensor_scalar(rstd[:, 2 * i:2 * i + 2], mv[:, 2 * i:2 * i + 2, 1], EPS, None,
                                        ALU.add).then_inc(ln_stats, 1)

            def layer_norm(n, i, b):
                dve.wait_ge(ln_rstd, 2 * n + i + 1)
                for q in (2 * i, 2 * i + 1):
                    nc.vector.tensor_scalar(tails[b].hn[:, q, :], tails[b].h[:, q, :], mv[:, q, 0:1], rstd[:, q:q + 1],
                                            ALU.subtract, ALU.mult).then_inc(ln_done, 1)

            def stage(name, b):
                key = (name, b)
                if name in ("SQ0", "SK0", "SQ1", "SK1") and b == 0:
                    i, half = int(name[1] == "K"), int(name[2])
                    wait_drained(dve, ("F" + name[1:], b))
                    vlink(nc.vector.tensor_copy(split[:, i, 0, half, :], qkf[:, i, :]))
                    vlink(nc.vector.tensor_tensor(qkf[:, i, :], qkf[:, i, :], split[:, i, 0, half, :], ALU.subtract))
                    vlink(nc.vector.tensor_copy(split[:, i, 1, half, :], qkf[:, i, :]))
                    nc.vector.tensor_tensor(split[:, i, 2, half, :], qkf[:, i, :], split[:, i, 1, half, :],
                                            ALU.subtract).then_inc(qk_parts, 1)
                elif name == "MT":
                    wait_full(dve, key)
                    if b:
                        dve.wait_ge(m_rows, 32 * b)
                    inc_drained(nc.vector.tensor_copy(mrows[:, :], bank(key)[:, 0:P // 2].bitcast(BF16)[0:2 * GS, :]), key)
                elif name == "NR":
                    wait_full(dve, key)
                    g = b % NG
                    if b:
                        wait_drained(dve, ("NR", b - 1))
                    if g == 0 and b:
                        wait_full(dve, ("VT1", b // NG - 1))
                    o = bank(key)[:, :].rearrange("p (q j c) -> p q j c", q=QT, j=HG)
                    vlink(nc.vector.reciprocal(rsum[:, :, :], o[:, :, :, HD]))
                    r = repeat(rsum[:, :, :].rearrange("p q (j a) -> p q j a", a=1), 3, HD)
                    dst = vals[:, :, HG * HD * g:HG * HD * (g + 1)].rearrange("p q (j c) -> p q j c", j=HG)
                    inc_drained(nc.vector.tensor_tensor(dst, o[:, :, :, 0:HD], r, ALU.mult), key)
                elif name in ("OP0", "OP1"):
                    wait_full(dve, key)
                    i = int(name[2])
                    if 0 < b < B - 1:
                        wait_drained(dve, ("V1", b - 1))
                        wait_drained(dve, ("V0", b - 1))
                    bb = repeat(w("bout").rearrange("p (a n) -> p a n", a=1), 1, 2)
                    inc_drained(nc.vector.tensor_tensor(tails[b].h[:, 2 * i:2 * i + 2, :],
                                                        bank(key)[:, :].rearrange("p (a n) -> p a n", a=2), bb, ALU.add), key)
                    if b:
                        dve.wait_ge(ln_done, QT * 2 * b)
                    layer_norm_stats(key, i, b)
                elif name == "LA":
                    if 0 < b < B - 1:
                        dve.wait_ge(out_done, 32 * b)
                    if b + 2 < B:
                        dve.wait_ge(x_low, KC * (b + 2))
                    layer_norm(2 * b, 0, b)
                    layer_norm(2 * b, 1, b)
                elif name[:2] in PAIRS:
                    ft = int(name[2])
                    dve.wait_ge(t_high, highs[key])
                    high, low = vT if name[:2] == "VT" else tails[b].hT
                    inc_drained(nc.vector.tensor_tensor(low[:, ft, :], bank(key)[:, :], high[:, ft, :], ALU.subtract), key)
                elif name in ("RQ0", "RQ1", "RK0", "RK1"):
                    wait_full(dve, key)
                    ft = int(name[2])
                    if b:
                        wait_full(dve, ("Y1", b - 1))
                        dve.wait_ge(qblk_in, 64 * b)
                        if name[1] == "K":
                            wait_full(dve, ("A13", b - 1))
                    table, dst = (gq, tails[b].rqT) if name[1] == "Q" else (gk, tails[b].rkT)
                    table = repeat(table[:, ft, :].rearrange("p (a n) -> p a n", a=1), 1, QT)
                    inc_drained(nc.vector.tensor_tensor(dst[:, ft, :].rearrange("p (a n) -> p a n", a=QT),
                                                        bank(key)[:, :].rearrange("p (a n) -> p a n", a=QT),
                                                        table, ALU.mult), key)
                elif name in ("KV0", "KV1"):
                    wait_full(dve, key)
                    if b:
                        dve.wait_ge(states, KC * b)
                    ft = int(name[2])
                    mask = repeat(w("gblocks", KC)[:, ft:ft + 1, :], 1, 3)
                    inc_drained(nc.vector.tensor_tensor(kvm[:, ft, :, :],
                                                        bank(key)[:, 0:3 * P].rearrange("p (a n) -> p a n", a=3),
                                                        mask, ALU.mult), key)
                elif name == "SS":
                    for n in ("KV0", "KV1"):
                        wait_drained(dve, (n, b))
                    if b:
                        wait_full(dve, ("Y1", b - 1))
                    else:
                        wait_drained(dve, ("C3", 0))
                    wait_full(dve, ("HT1", b))
                    for c in range(3):
                        for ft in range(KC):
                            ins = nc.vector.scalar_tensor_tensor(
                                out=tails[b].state[c + 1][:, ft, :], in0=tails[b].state[c][:, ft, :], scalar=w("gchunk")[:, ft:ft + 1],
                                in1=kvm[:, ft, c, :], op0=ALU.mult, op1=ALU.add)
                            ins.then_inc(states if c == 2 else v_chain, 1)
                        if c < 2:
                            vcount[0] += KC
                            dve.wait_ge(v_chain, vcount[0])
                elif name[0] == "A":
                    ft, c = int(name[1]), int(name[2])
                    wait_full(dve, key)
                    chunk = QT * ft + c
                    if chunk >= 2:
                        last_ft, last_c = divmod(chunk - 2, QT)
                        if last_c == QT - 1:
                            wait_full(dve, (f"Y{last_ft}", b))
                        else:
                            dve.wait_ge(y_chunk, 3 * (2 * b + last_ft) + last_c + 1)
                    else:
                        dve.wait_ge(qk_parts, 4 * min(b + 3, B))
                        if b:
                            wait_full(dve, ("Y1", b - 1))
                    mask = repeat(w("causal").rearrange("p (a n) -> p a n", a=1), 1, RQ)
                    inc_drained(nc.vector.tensor_tensor(amask[:, c % 2, :, :],
                                                        bank(key)[:, :].rearrange("p (a n) -> p a n", a=RQ),
                                                        mask, ALU.mult), key)
                elif name in ("Y03", "Y13"):
                    ft = int(name[1])
                    wait_drained(dve, (name[:2], b))
                    if b == 0 and ft == 0:
                        wait_drained(dve, ("C4", 0))
                    if b:
                        dve.wait_ge(g_dev, b)
                        dve.wait_ge(z_done, KC * b)
                    vlink(nc.vector.tensor_copy(y[:, ft, S:S + 1], yc[:, ft:ft + 1]))
                    half = (S + 2) // 2
                    nc.vector.bn_stats(gst[:, ft, 0, :], y[:, ft, 0:half]).then_inc(v_chain, 1)
                    nc.vector.bn_stats(gst[:, ft, 1, :], y[:, ft, half:S + 1]).then_inc(v_chain, 1)
                    vcount[0] += 2
                    dve.wait_ge(v_chain, vcount[0])
                    last = nc.vector.bn_aggr(gmv[:, ft, :], gst[:, ft, :, :].rearrange("p a b -> p (a b)"))
                    if ft:
                        last.then_inc(g_mean, 1)
                    else:
                        vlink(last)
                elif name == "GM":
                    wait_full(dve, key)
                    dve.wait_ge(g_mean, b + 1)
                    if b:
                        dve.wait_ge(z_done, KC * b)
                        wait_full(dve, ("GV", b - 1))
                    inc_drained(nc.vector.tensor_copy(gmu[:, :], bank(key)[:, 0:KC]), key)
                    wait_drained(dve, key)
                    vlink(nc.vector.tensor_tensor(gvar[:, :], gmv[:, :, 0], gmu[:, :], ALU.subtract))
                    vlink(nc.vector.tensor_tensor(gvar[:, :], gvar[:, :], gvar[:, :], ALU.mult))
                    nc.vector.tensor_tensor(gd[:, :], gvar[:, :], gmv[:, :, 1], ALU.add).then_inc(g_dev, 1)
                elif name == "GV":
                    wait_full(dve, key)
                    dve.wait_ge(g_dev, b + 1)
                    inc_drained(nc.vector.tensor_scalar(gvar[:, :], bank(key)[:, 0:KC], EPS, None, ALU.add), key)
                elif name == "GZ":
                    dve.wait_ge(g_rstd, b + 1)
                    vlink(nc.vector.tensor_tensor(gscale[:, :], grs[:, :], w("gnw"), ALU.mult))
                    vlink(nc.vector.tensor_tensor(gmu[:, :], gmu[:, :], gscale[:, :], ALU.mult))
                    vlink(nc.vector.tensor_tensor(gshift[:, :], w("gnb"), gmu[:, :], ALU.subtract))
                    wait_full(dve, ("OP1", b))
                    for ft in range(KC):
                        nc.vector.tensor_scalar(y[:, ft, :], y[:, ft, :], gscale[:, ft:ft + 1], gshift[:, ft:ft + 1],
                                                ALU.mult, ALU.add).then_inc(z_whole, 1)
                    for ft in range(KC):
                        dve.wait_ge(z_high, KC * b + ft + 1)
                        nc.vector.tensor_tensor(z[1][:, ft, :], y[:, ft, :], z[0][:, ft, :],
                                                ALU.subtract).then_inc(z_done, 1)
                elif name in ("WO0", "WO1"):
                    wait_full(dve, key)
                    dve.wait_ge(ln_done, QT * (2 * b + 1))
                    i = int(name[2])
                    hv = tails[b].h[:, 2 * i:2 * i + 2, :].rearrange("p a b -> p (a b)")
                    inc_drained(nc.vector.tensor_tensor(hv, bank(key)[:, :], hv, ALU.add), key)
                    layer_norm_stats(key, i, b)
                elif name == "LB":
                    wait_full(dve, ("HT1", b))
                    layer_norm(2 * b + 1, 0, b)
                    layer_norm(2 * b + 1, 1, b)
                elif name == "U1":
                    wait_full(dve, key)
                    if b:
                        wait_full(dve, ("H7", b - 1))
                    up = slice(P // 2, P)
                    vlink(nc.vector.tensor_copy(p_parts[:, :], bank(key)[:, :]))
                    inc_drained(nc.vector.tensor_tensor(p_parts[up, :], bank(key)[up, :], p_parts[up, :], ALU.subtract), key)
                elif name in ("V0", "V1"):
                    wait_full(dve, key)
                    dve.wait_ge(hb_done, b + 1)
                    wait_full(dve, ("HU1", b))
                    i = int(name[1])
                    inc_drained(nc.vector.tensor_tensor(tails[b].hn[:, 2 * i:2 * i + 2, :].rearrange("p a b -> p (a b)"),
                                                        bank(key)[:, :], tails[b].h[:, 2 * i:2 * i + 2, :].rearrange("p a b -> p (a b)"),
                                                        ALU.add), key)
                elif name == "C0":
                    wait_full(dve, key)
                    inc_drained(nc.vector.tensor_copy(cT[:, 0, :], bank(key)[:, 0:KC]), key)
                elif name == "C1":
                    wait_full(dve, key)
                    inc_drained(nc.vector.tensor_copy(cT[:, 1, :], bank(key)[:, 0:KC]), key)
                elif name == "C2":
                    wait_full(dve, key)
                    inc_drained(nc.vector.tensor_copy(crow[0:1, 1:3, :].rearrange("p a b -> p (a b)"), bank(key)[0:1, :]), key)
                elif name == "C3":
                    wait_full(dve, key)
                    mask = repeat(w("blocks").rearrange("p (a n) -> p a n", a=1), 1, KC)
                    inc_drained(nc.vector.tensor_tensor(tails[b].state[0],
                                                        bank(key)[:, 0:KC * P].rearrange("p (a n) -> p a n", a=KC),
                                                        mask, ALU.mult), key)
                elif name == "C4":
                    wait_full(dve, key)
                    inc_drained(nc.vector.tensor_copy(yc[:, :], bank(key)[:, 0:KC]), key)
                elif name == "CW":
                    wait_full(dve, key)
                    dve.wait_ge(cls_in, 32)
                    inc_drained(nc.vector.tensor_tensor(crow_end[:, 3, :], bank(key)[0:B, 0:D], clsrow_end, ALU.add), key)
                    wait_drained(dve, key)
                    dve.wait_ge(c_hn, 1)
                    row_stats(crow_end[:, 3, :], B)
                    row_norm(crow_end[:, 3, :], crow_end[:, 0, :], B, 2)
                elif name == "CT":
                    wait_full(dve, key)
                    column = bank(key)[:, 0:KC * B].rearrange("p (a b) -> p a b", a=KC)
                    vlink(nc.vector.tensor_copy(cTp[:, 0], column))
                    inc_drained(nc.vector.tensor_tensor(cTp[:, 1], column, cTp[:, 0], ALU.subtract), key)
                elif name == "CU":
                    wait_full(dve, key)
                    up = slice(P // 2, P)
                    vlink(nc.vector.tensor_copy(cP[:, :], bank(key)[:, 0:B]))
                    inc_drained(nc.vector.tensor_tensor(cP[up, :], bank(key)[up, 0:B], cP[up, :], ALU.subtract), key)
                elif name == "CH":
                    wait_full(dve, key)
                    bb = repeat(w("b1").rearrange("p (f a) -> p f a", a=1), 2, B)
                    inc_drained(nc.vector.tensor_tensor(chid, bank(key)[:, 0:FT * B].rearrange("p (f a) -> p f a", a=B),
                                                        bb, ALU.add), key)
                elif name == "CQ":
                    wait_full(dve, key)
                    inc_drained(nc.vector.tensor_copy(cQ, bank(key)[:, 0:B]), key)
                elif name == "CV":
                    wait_full(dve, key)
                    vlink(nc.vector.tensor_tensor(crow_end[:, 1, :], bank(key)[0:B, 0:D], crow_end[:, 3, :], ALU.add))
                    nc.vector.tensor_tensor(crow_end[:, 2, :], crow_end[:, 1, :], w("b2")[0:B, :], ALU.add).then_inc(c_out, 1)

            for it, t, step, todo in walk:
                m = step + AHEAD
                if 0 <= m < B * STEPS:
                    n = m // GS
                    dve.wait_ge(max_full, m + 1)
                    if n >= 2 and m % GS == 0:
                        dve.wait_ge(m_split, n - 1)
                    nc.vector.tensor_reduce(negmax[:, n % 2, m % GS:m % GS + 1], mx_ps[:, m % 2, :], AX, ALU.max,
                                            negate=True).then_inc(max_done, 1)
                    if m % GS == GS - 1:
                        dve.wait_ge(max_done, m + 1)
                        if n:
                            wait_full(dve, ("MT", n - 1))
                        vlink(nc.vector.tensor_copy(mparts[:, 0, :], negmax[:, n % 2, :]))
                        nc.vector.tensor_tensor(mparts[:, 1, :], negmax[:, n % 2, :], mparts[:, 0, :],
                                                ALU.subtract).then_inc(m_split, 1)
                if step == CLASS_NORM:
                    class_norm()
                for name, b in todo:
                    stage(name, b)

        @block.gpsimd
        def _(pool):
            nc.gpsimd.memset(kr[KR:KM, :, :], 1.0).then_inc(ones_done, 1)
            pool.wait_ge(ones_done, 1)
            nc.gpsimd.memset(mhalf[:, :], -0.5).then_inc(halves_set, 1)
            nc.gpsimd.memset(one[:, :], 1.0).then_inc(halves_set, 1)
            nc.gpsimd.memset(vaug[:, :, :, HD:32], 0.0).then_inc(vconst, 1)
            pool.wait_ge(vconst, 1)
            nc.gpsimd.memset(vaug[:, :, :, HD:HD + 1], 1.0).then_inc(vconst, 1)
            nc.gpsimd.memset(qblk[:, :, :, :], 0.0).then_inc(zeros_done, 1)

            def class_rstd(n, count):
                pool.wait_ge(c_var, count)
                pool.wait_ge(halves_set, 2)
                nc.gpsimd.tensor_tensor(cmv[0:n, 3:4], cmv[0:n, 2:3], mhalf[0:n, 0:1], ALU.pow).then_inc(c_rstd, 1)

            def layer_norm_rstd(n, i):
                pool.wait_ge(ln_stats, 2 * n + i + 1)
                at = slice(2 * i, 2 * i + 2)
                nc.gpsimd.tensor_tensor(rstd[:, at], rstd[:, at], mhalf[:, at], ALU.pow).then_inc(ln_rstd, 1)

            for it, t, step, todo in walk:
                for i, at in enumerate(W_SPLIT):
                    if step == at:
                        pool.wait_ge(w_high, i + 1)
                        name = WEIGHTS[i][0]
                        high, low = (part[:, woff[name]] for part in weight_parts)
                        nc.gpsimd.tensor_tensor(low, whole(name), high, ALU.subtract).then_inc(w_low, 1)
                if step == CLASS_NORM:
                    class_rstd(1, 1)
                for half in range(2):
                    b = it + 1 - half
                    if step == V_COPY_FIRST[half]:
                        b = 0
                    if step == V_COPY_FIRST[half] or t == V_COPY[half] and 1 <= b < B:
                        wait_drained(pool, ("FV0", b))
                        wait_drained(pool, ("FV1", b))
                        pool.wait_ge(vconst, 2)
                        if b:
                            pool.wait_ge(pv_done, QT * (NG * b - (NG // 2 if half == 0 else 0)))
                        pool.wait_ge(small_in, 16)
                        heads, features = slice(HH * half, HH * (half + 1)), slice(HH * HD * half, HH * HD * (half + 1))
                        bias = repeat(w("vbias")[:, features].rearrange("p (a h d) -> p a h d", a=1, d=HD), 1, QT)
                        nc.gpsimd.tensor_tensor(vaug[:, :, heads, 0:HD],
                                                vstage[:, :, features].rearrange("p q (h d) -> p q h d", d=HD),
                                                bias, ALU.add)\
                            .then_inc(v_half, 1)
                for name, b in todo:
                    if name == "XS" and b:
                        for k in range(KC):
                            pool.wait_ge(x_high, KC * (b - 1) + k + 1)
                            nc.gpsimd.tensor_tensor(x_parts[1][:, k, :], xT[:, k, :], x_parts[0][:, k, :],
                                                    ALU.subtract).then_inc(x_low, 1)
                    elif name in ("FQ0", "FK0", "FQ1", "FK1") and b:
                        i, half = int(name[1] == "K"), int(name[2])
                        wait_drained(pool, (name, b))
                        pool.wait_ge(first_part, 4 * (b - 1) + 2 * half + i + 1)
                        nc.gpsimd.tensor_tensor(qkf[:, i, :], qkf[:, i, :], split[:, i, 0, half, :],
                                                ALU.subtract).then_inc(qk_rest, 1)
                    elif name in ("SQ0", "SK0", "SQ1", "SK1") and b:
                        i, half = int(name[1] == "K"), int(name[2])
                        pool.wait_ge(second_part, 4 * (b - 1) + 2 * half + i + 1)
                        pool.wait_ge(qk_parts, 4 * b + 2 * half + i)
                        nc.gpsimd.tensor_tensor(split[:, i, 2, half, :], qkf[:, i, :], split[:, i, 1, half, :],
                                                ALU.subtract).then_inc(qk_parts, 1)
                    elif name in ("OP0", "OP1"):
                        layer_norm_rstd(2 * b, int(name[2]))
                    elif name == "GV":
                        wait_drained(pool, ("GV", b))
                        if b:
                            pool.wait_ge(z_done, KC * b)
                        nc.gpsimd.tensor_tensor(grs[:, :], gvar[:, :], mhalf[:, 0:KC], ALU.pow).then_inc(g_rstd, 1)
                        pool.wait_ge(z_done, KC * (b + 1))
                        for i in range(2):
                            nc.gpsimd.tensor_scalar(zc[:, i, :, b], z[i][:, :, S], 1.0, None, ALU.mult).then_inc(zc_done, 1)
                    elif name == "WO0":
                        layer_norm_rstd(2 * b + 1, 0)
                    elif name == "WO1":
                        layer_norm_rstd(2 * b + 1, 1)
                    elif name == "LB":
                        pool.wait_ge(ln_done, QT * (2 * b + 2))
                        bb = repeat(w("b2").rearrange("p (a n) -> p a n", a=1), 1, QT)
                        nc.gpsimd.tensor_tensor(tails[b].h[:, :, :], tails[b].h[:, :, :], bb, ALU.add).then_inc(hb_done, 1)
                    elif name == "CW":
                        class_rstd(B, 2)


def kernel(**inputs):
    import numpy as np
    import concourse.bacc as bacc
    from concourse.bass_utils import run_bass_kernel_spmd as run

    a = {k: np.asarray(v) for k, v in inputs.items()}
    f32 = np.float32

    def tiles(m):
        return np.ascontiguousarray(m.reshape(-1, P, m.shape[1]).transpose(1, 0, 2)).reshape(P, -1)

    def column(v):
        return np.ascontiguousarray(v.reshape(-1, P).T)

    def everywhere(v):
        return np.broadcast_to(v, (P, v.size))

    wqkv = a["L0_tok_w_qkv"].reshape(2, HH, 3, HD, D)
    bqkv = a["L0_tok_b_qkv"].reshape(2, HH, 3, HD)
    pick = lambda i: (wqkv[:, :, i].transpose(0, 2, 1, 3).reshape(D, D).T, bqkv[:, :, i].transpose(0, 2, 1).reshape(D))
    (wq, bq), (wk, bk) = pick(0), pick(1)
    wv, bv = wqkv[:, :, 2].reshape(D, D).T, bqkv[:, :, 2].reshape(D)
    v = {
        "wq": tiles(wq), "wk": tiles(wk), "wv": tiles(wv),
        "qbias": column(bq), "kbias": column(bk),
        "vbias": everywhere(bv), "ident": np.eye(P, dtype=f32),
        "wout": tiles(a["L0_tok_w_out"].T), "bout": everywhere(a["L0_tok_b_out"]),
        "rwq": tiles(a["L0_attn_Wq"].T), "rwk": tiles(a["L0_attn_Wk"].T), "rwv": tiles(a["L0_attn_Wv"].T),
        "rwo": tiles(a["L0_attn_Wo"].T), "gnw": column(a["L0_attn_gn_weight"]), "gnb": column(a["L0_attn_gn_bias"]),
        "u1": tiles(np.concatenate([a["L0_ffn_U1"]] * 2, axis=1)), "b1": column(a["L0_ffn_b1"]), "u2": tiles(a["L0_ffn_U2"]), "v2": np.concatenate([a["L0_ffn_V2"]] * 2),
        "v1": np.concatenate([a["L0_ffn_V1"]] * 2), "b2": everywhere(a["L0_ffn_b2"]),
    }
    decay = (f32(1) - np.exp(np.linspace(np.log(1 / 32), np.log(1 / 512), RH).astype(f32))).astype(np.float64)
    by_feature = np.repeat(decay, RD)[:, None]
    power = by_feature ** np.arange(1, P + 1)[None]
    v["gq"], v["gk"] = tiles(power.astype(f32)), tiles((1 / power).astype(f32))
    v["gchunk"] = tiles((by_feature ** P).astype(f32))
    i = np.arange(P)
    v["causal"] = (i[:, None] <= i[None]).astype(f32)
    v["blocks"] = (i[:, None] // RD == i[None] // RD).astype(f32)
    v["gblocks"] = (np.tile(v["blocks"], (1, KC)).reshape(P, KC, P) * v["gchunk"][:, :, None]).reshape(P, KC * P)
    v["headmean"] = v["blocks"] * f32(1 / RD)
    arrays = {
        "xt": np.ascontiguousarray(a["x"].reshape(B, S, KC, P).transpose(0, 3, 2, 1)),
        "front_weights": np.concatenate([v[n] for n, _ in FRONT_WEIGHTS], axis=1),
        "front": np.concatenate([v[n] for n, _ in FRONT], axis=1),
        "rest": np.concatenate([v[n] for n, _ in REST], axis=1),
        "weights": np.concatenate([v[n] for n, _ in WEIGHTS[len(FRONT_WEIGHTS):]], axis=1),
        "cls": np.ascontiguousarray(np.broadcast_to(a["cls_tok"].reshape(1, D), (B, D))),
    }
    nc = bacc.Bacc("TRN2", target_bir_lowering=False, num_devices=1)
    args = [nc.dram_tensor(n, m.shape, mybir.dt.from_np(m.dtype), kind="ExternalInput").ap() for n, m in arrays.items()]
    out = nc.dram_tensor("out_0_dram", (B, S + 1, D), F32, kind="ExternalOutput").ap()
    vit_tower(nc, *args, out)
    return run(nc, [arrays], core_ids=[0]).results[0]["out_0_dram"]
```
